# Optimizing a Trainium2 kernel written in Bass

```python
import numpy as np
import jax
import jax.numpy as jnp

def _softmax(x, axis=-1):
    return jax.nn.softmax(x, axis=axis)

def _gelu(x):
    return jax.nn.gelu(x, approximate=True)

def _silu(x):
    return jax.nn.silu(x)

def _sigmoid(x):
    return jax.nn.sigmoid(x)

def _layernorm(x, axis=-1, eps=1e-05):
    m = jnp.mean(x, axis=axis, keepdims=True)
    v = jnp.var(x, axis=axis, keepdims=True)
    return (x - m) / jnp.sqrt(v + eps)

def _scatter_add(tgt, idx, src, axis=0):
    return tgt.at[idx].add(src)

def _segment_sum(src, seg, n):
    return jax.ops.segment_sum(src, seg, n)
kernel_name = 'mk_flamingo_gated_d1_seqx_r8_f839dc'

def setup_inputs(seed: int=0):
    np.random.seed(seed)
    _w = jnp.asarray

    def _rec_inputs():
        import jax
        import jax.numpy as jnp
        _rk = jax.random.key(seed)
        x = 7.22e-05 + 1 * jax.random.normal(jax.random.fold_in(_rk, 1), (128, 64, 128), jnp.float32)
        _lenS = 64 - jax.random.randint(jax.random.fold_in(_rk, 7), (128,), 0, max(1, 64 // 4) + 1, jnp.int32)
        _lenS2 = 64 - jax.random.randint(jax.random.fold_in(_rk, 8), (128,), 0, max(1, 64 // 4) + 1, jnp.int32)
        _ctx_1024P = jax.random.normal(jax.random.fold_in(_rk, 11), (128, 16, 128), jnp.float32)
        _ctx_1024c = jax.random.dirichlet(jax.random.fold_in(_rk, 511), 0.3 * jnp.ones((16,), jnp.float32), (128, 64))
        _ctx_1024t = jnp.einsum('bsk,bkd->bsd', _ctx_1024c, _ctx_1024P)
        _ctx_1024t = _ctx_1024t * jax.lax.rsqrt(jnp.mean(jnp.square(_ctx_1024t)) + 1e-12) * 0.953939
        ctx_1024 = 4.13588e-05 + 0.999923 * (_ctx_1024t + 0.3 * jax.random.normal(jax.random.fold_in(_rk, 611), (128, 64, 128), jnp.float32))
        _g = jax.random.normal(jax.random.fold_in(_rk, 9001), (2, 1), jnp.float32)
        _g = jnp.sign(_g) * jnp.maximum(jnp.abs(_g), 1.0) + (_g == 0) * 1.0
        g_xattn = _g[0]
        g_ffn = _g[1]
        return (x, ctx_1024, g_xattn, g_ffn)
    x, ctx_1024, g_xattn, g_ffn = _rec_inputs()

    def _L0_xattn_setup():
        import jax, jax.numpy as jnp
        import numpy as np
        D_MODEL = 128
        NUM_HEADS = 16
        HEAD_DIM = D_MODEL // NUM_HEADS
        MAX_SEQ = 64

        def rope_tables(seq_len, dim):
            inv_freq = 1.0 / 10000.0 ** (jnp.arange(0, dim, 2, dtype=jnp.float32) / dim)
            t = jnp.arange(seq_len, dtype=jnp.float32)
            freqs = jnp.einsum('i,j->ij', t, inv_freq)
            emb = jnp.concatenate([freqs, freqs], axis=-1)
            return (jnp.cos(emb), jnp.sin(emb))

        def rotate_half(x):
            x1, x2 = jnp.split(x, 2, axis=-1)
            return jnp.concatenate([-x2, x1], axis=-1)
        key = jax.random.key(seed)
        ks = jax.random.split(key, 12)
        B, S, D = (16, 64, D_MODEL)
        s = 1.0 / np.sqrt(D)
        inp = {'query': jax.random.normal(ks[0], (B, S, D), jnp.float32), 'key': jax.random.normal(ks[1], (B, S, D), jnp.float32), 'value': jax.random.normal(ks[2], (B, S, D), jnp.float32), 'Wq': jax.random.normal(ks[3], (D, D), jnp.float32) * s, 'bq': jnp.zeros((D,), jnp.float32), 'Wk': jax.random.normal(ks[4], (D, D), jnp.float32) * s, 'bk': jnp.zeros((D,), jnp.float32), 'Wv': jax.random.normal(ks[5], (D, D), jnp.float32) * s, 'bv': jnp.zeros((D,), jnp.float32), 'Wo': jax.random.normal(ks[6], (D, D), jnp.float32) * s, 'bo': jnp.zeros((D,), jnp.float32)}
        return inp
    _L0_xattn_all = _L0_xattn_setup()
    _L0_xattn_in = {k: v for k, v in _L0_xattn_all.items() if k in ('Wq', 'bq', 'Wk', 'bk', 'Wv', 'bv', 'Wo', 'bo')}
    del _L0_xattn_all

    def _L0_ffn_setup():
        import jax, jax.numpy as jnp
        import numpy as np
        E, TOP_K, D, H = (8, 2, 128, 256)
        B, S = (2, 256)
        key = jax.random.key(seed)
        ks = jax.random.split(key, 10)
        s = 0.02
        return {'x': jax.random.normal(ks[0], (B, S, D), dtype=jnp.float32), 'gate_w': jax.random.normal(ks[1], (E, D), dtype=jnp.float32) * s, 'gate_b': jnp.zeros((E,), dtype=jnp.float32), 'w0': jax.random.normal(ks[2], (E, H, D), dtype=jnp.float32) * s, 'b0': jnp.zeros((E, H), dtype=jnp.float32), 'w1': jax.random.normal(ks[3], (E, H, D), dtype=jnp.float32) * s, 'b1': jnp.zeros((E, H), dtype=jnp.float32), 'w2': jax.random.normal(ks[4], (E, D, H), dtype=jnp.float32) * s, 'b2': jnp.zeros((E, D), dtype=jnp.float32)}
    _L0_ffn_all = _L0_ffn_setup()
    _L0_ffn_in = {k: v for k, v in _L0_ffn_all.items() if k in ('gate_w', 'gate_b', 'w0', 'b0', 'w1', 'b1', 'w2', 'b2')}
    del _L0_ffn_all
    return {'x': x, 'ctx_1024': ctx_1024, 'g_xattn': g_xattn, 'g_ffn': g_ffn, 'L0_xattn_Wq': _L0_xattn_in['Wq'], 'L0_xattn_bq': _L0_xattn_in['bq'], 'L0_xattn_Wk': _L0_xattn_in['Wk'], 'L0_xattn_bk': _L0_xattn_in['bk'], 'L0_xattn_Wv': _L0_xattn_in['Wv'], 'L0_xattn_bv': _L0_xattn_in['bv'], 'L0_xattn_Wo': _L0_xattn_in['Wo'], 'L0_xattn_bo': _L0_xattn_in['bo'], 'L0_ffn_gate_w': _L0_ffn_in['gate_w'], 'L0_ffn_gate_b': _L0_ffn_in['gate_b'], 'L0_ffn_w0': _L0_ffn_in['w0'], 'L0_ffn_b0': _L0_ffn_in['b0'], 'L0_ffn_w1': _L0_ffn_in['w1'], 'L0_ffn_b1': _L0_ffn_in['b1'], 'L0_ffn_w2': _L0_ffn_in['w2'], 'L0_ffn_b2': _L0_ffn_in['b2']}

def reference(x, ctx_1024, g_xattn, g_ffn, L0_xattn_Wq, L0_xattn_bq, L0_xattn_Wk, L0_xattn_bk, L0_xattn_Wv, L0_xattn_bv, L0_xattn_Wo, L0_xattn_bo, L0_ffn_gate_w, L0_ffn_gate_b, L0_ffn_w0, L0_ffn_b0, L0_ffn_w1, L0_ffn_b1, L0_ffn_w2, L0_ffn_b2):
    import jax
    import jax.numpy as jnp

    def _L0_xattn_ref(query, key, value, Wq, bq, Wk, bk, Wv, bv, Wo, bo):
        import jax, jax.numpy as jnp
        import numpy as np
        D_MODEL = 128
        NUM_HEADS = 16
        HEAD_DIM = D_MODEL // NUM_HEADS
        MAX_SEQ = 64

        def rope_tables(seq_len, dim):
            inv_freq = 1.0 / 10000.0 ** (jnp.arange(0, dim, 2, dtype=jnp.float32) / dim)
            t = jnp.arange(seq_len, dtype=jnp.float32)
            freqs = jnp.einsum('i,j->ij', t, inv_freq)
            emb = jnp.concatenate([freqs, freqs], axis=-1)
            return (jnp.cos(emb), jnp.sin(emb))

        def rotate_half(x):
            x1, x2 = jnp.split(x, 2, axis=-1)
            return jnp.concatenate([-x2, x1], axis=-1)
        B, S, D = query.shape
        H, Hd = (NUM_HEADS, HEAD_DIM)
        scale = Hd ** (-0.5)

        def proj(x, W, b):
            y = jnp.einsum('bsd,ed->bse', x, W) + b
            return y.reshape(B, S, H, Hd).transpose(0, 2, 1, 3)
        q = proj(query, Wq, bq)
        k = proj(key, Wk, bk)
        v = proj(value, Wv, bv)
        cos, sin = rope_tables(S, Hd)
        cos = cos[None, None]
        sin = sin[None, None]
        q = q * cos + rotate_half(q) * sin
        k = k * cos + rotate_half(k) * sin
        attn = jnp.einsum('bhqd,bhkd->bhqk', q, k) * scale
        attn_w = jax.nn.softmax(attn, axis=-1)
        out = jnp.einsum('bhqk,bhkd->bhqd', attn_w, v)
        out = out.transpose(0, 2, 1, 3).reshape(B, S, D)
        out = jnp.einsum('bsd,ed->bse', out, Wo) + bo
        return out

    def _L0_ffn_ref(x, gate_w, gate_b, w0, b0, w1, b1, w2, b2):
        import jax, jax.numpy as jnp
        import numpy as np
        E, TOP_K, D, H = (8, 2, 128, 256)
        B, S = (2, 256)
        Bn, Sq, Dv = x.shape
        xt = x.reshape(-1, Dv)
        logits = xt @ gate_w.T + gate_b
        top_v, top_i = jax.lax.top_k(logits, TOP_K)
        h0 = jnp.einsum('td,ehd->eth', xt, w0) + b0[:, None, :]
        h1 = jnp.einsum('td,ehd->eth', xt, w1) + b1[:, None, :]
        act = h0 * jax.nn.silu(h1)
        out_all = jnp.einsum('eth,edh->etd', act, w2) + b2[:, None, :]
        out_te = jnp.transpose(out_all, (1, 0, 2))
        sel = jnp.take_along_axis(out_te, top_i[:, :, None], axis=1)
        w = jax.nn.softmax(top_v, axis=-1)[:, :, None]
        out = (w * sel).sum(axis=1)
        return out.reshape(Bn, Sq, Dv)
    x = x + jnp.tanh(g_xattn[0]) * _L0_xattn_ref(_layernorm(x, axis=-1), ctx_1024, ctx_1024, L0_xattn_Wq, L0_xattn_bq, L0_xattn_Wk, L0_xattn_bk, L0_xattn_Wv, L0_xattn_bv, L0_xattn_Wo, L0_xattn_bo)
    x = x + jnp.tanh(g_ffn[0]) * _L0_ffn_ref(_layernorm(x, axis=-1), L0_ffn_gate_w, L0_ffn_gate_b, L0_ffn_w0, L0_ffn_b0, L0_ffn_w1, L0_ffn_b1, L0_ffn_w2, L0_ffn_b2)
    return x

_drawn_inputs = setup_inputs


def setup_inputs(seed=0):
    import zlib

    import numpy as np

    out = dict(_drawn_inputs(seed))
    spreads = {'L0_xattn_bq': (0.0, 0.419),
     'L0_xattn_bk': (0.0, 0.8),
     'L0_xattn_bv': (0.0, 0.1),
     'L0_xattn_bo': (0.0, 0.1),
     'L0_ffn_gate_b': (0.0, 0.1),
     'L0_ffn_b0': (0.0, 0.8),
     'L0_ffn_b1': (0.0, 0.8),
     'L0_ffn_b2': (0.0, 0.585)}
    factors = {'L0_ffn_w0': 8.0, 'L0_ffn_w1': 8.0, 'L0_ffn_w2': 8.0}
    for name, (base, spread) in spreads.items():
        noise = np.random.default_rng([zlib.crc32(name.encode()), seed]).standard_normal(out[name].shape)
        drawn = base * np.exp(spread * noise) if base else spread * noise
        out[name] = jnp.asarray(drawn.astype(out[name].dtype))
    for name, factor in factors.items():
        out[name] = (out[name] * factor).astype(out[name].dtype)
    return out
```

```python
from contextlib import ExitStack

import numpy as np

import concourse.bass as bass
from concourse import mybir

F32 = mybir.dt.float32
BF16 = mybir.dt.bfloat16
I32 = mybir.dt.int32
U32 = mybir.dt.uint32
ALU = mybir.AluOpType
ACT = mybir.ActivationFunctionType
AX = mybir.AxisListType.X

P = 128
D = 128
B, S = 128, 64
NH, HD = 16, 8
E, H = 8, 256
T = B * S // P
TOKENS = T * P
EPS = 1e-5
SCALE = HD ** -0.5

REGION = TOKENS + P
ROW = D + 2
BLOCKS = (2 * TOKENS + E * (P - 1)) // P + 1
BLOCKS += -BLOCKS % 8
NOWHERE = 2 * TOKENS

NORM1, TURN, VALUE, SCORE, PROB, WO, GATE, ROUTE, SCATTER = 0, 1, 2, 4, 5, 6, 7, 8, 9
FILL = 12
ROWS_T, HIDDEN, ACT_T, RESULT = 0, 1, 2, 3
BLOCK_DRAIN = 4


def tile(ii, k, lag):
    return 4 * ii + (k - lag)


def runs(ii, k, lag):
    return not isinstance(ii, int) or 0 <= 4 * ii + k - lag < T


def steps(engine, step):
    for k in range(FILL):
        step(0, k)
    with engine.Fori(FILL // 4, T // 4) as ii:
        for k in range(4):
            step(ii, k)
    for k in range(SCATTER):
        step(T // 4, k)


def block_steps(engine, step):
    for k in range(8):
        step(0, k)
    with engine.Fori(1, BLOCKS // 8) as ii:
        for k in range(8):
            step(ii, k)
    for k in range(BLOCK_DRAIN):
        step(BLOCKS // 8, k)


def block(ii, k, lag):
    return 8 * ii + (k - lag)


def block_runs(ii, k, lag):
    return not isinstance(ii, int) or 0 <= 8 * ii + k - lag < BLOCKS


def flamingo_block(nc, a, out):
    with ExitStack() as ctx:
        def sb(name, shape, dt=F32):
            return ctx.enter_context(nc.sbuf_tensor(name, shape, dt))

        def sem(name):
            return ctx.enter_context(nc.semaphore(name))

        rows_dram = nc.dram_tensor("rows_by_expert", [E * REGION + P, ROW], F32, kind="Internal").ap()
        result_dram = nc.dram_tensor("results_by_slot", [2 * TOKENS, D], F32, kind="Internal").ap()

        ident = sb("ident", [P, P])
        before = sb("before", [P, 2, P], BF16)
        head_mask = sb("head_mask", [P, 8])
        mask_by_b = sb("mask_by_b", [P, 2, 8])
        iota8 = sb("iota8", [P, 2, E])
        half = sb("half", [P, 1])
        wq = sb("wq", [P, 2, D])
        wk = sb("wk", [P, 2, D])
        wv = sb("wv", [P, D])
        wo = sb("wo", [P, D])
        wo_gated = sb("wo_gated", [P, D])
        turn_tab = sb("turn_tab", [P, 2, S])
        qb_col = sb("qb_col", [P, 2, 2])
        kb_col = sb("kb_col", [P, 2, 2])
        qb_tab = sb("qb_tab", [P, 2, 2, S])
        kb_tab = sb("kb_tab", [P, 2, 2, S])
        bt_tmp = sb("bt_tmp", [P, 2, S])
        bv_col = sb("bv_col", [P, 1])
        bv_wide = sb("bv_wide", [P, P])
        bo_wide = sb("bo_wide", [P, D])
        gates = sb("gates", [P, 2])
        tgate = sb("tgate", [P, 2])
        gate_w = sb("gate_w_sb", [P, E])
        gate_b = sb("gate_b_sb", [P, E])
        w01 = sb("w01", [P, E * 2 * H])
        b01 = sb("b01", [P, E * 2 * H])
        w2 = sb("w2_sb", [P, E * 2 * D])
        b2 = sb("b2_sb", [P, E * D])

        x = sb("x_sb", [P, T, D])
        ctx_in = sb("ctx_in", [P, 4, D])
        stats1 = sb("stats1", [P, 4, 6])
        mv1 = sb("mv1", [P, 4, 2])
        rstd1 = sb("rstd1", [P, 4, 2])
        xn = sb("xn", [P, 2, D])
        turned = sb("turned", [P, 4, 4, P])
        rope_mul = sb("rope_mul", [P, 2, 2, 2, S])
        rope_sum = sb("rope_sum", [P, 2, 2, S])
        k_rot = sb("k_rot", [P, 2, 2, S])[:]
        k_bd = sb("k_bd", [P, 2, 2, 2, 8, S])
        q_bd = sb("q_bd", [P, 2, 2, 2, 2, S])
        peak = sb("peak", [P, 2, NH])
        probs = sb("probs", [P, 2, 2, 8, S])
        probs_t = sb("probs_t", [P, 2, 8, P])
        v_bd = sb("v_bd", [P, 4, 2, 8, 32])
        mixed = sb("mixed", [P, 2, 2, P])
        inv = sb("inv", [P, 2, NH])
        o = sb("o_sb", [P, 2, D])
        stats2 = sb("stats2", [P, 4, 6])
        mv2 = sb("mv2", [P, 4, 2])
        rstd2 = sb("rstd2", [P, 4, 2])
        routed = sb("routed", [P, 4, 2, ROW])
        logits = sb("logits", [P, 2, E])
        top = sb("top", [P, 2, 8])
        top_at = sb("top_at", [P, 2, 8], U32)
        top_f = sb("top_f", [P, 2, 2])
        chosen = sb("chosen", [P, 2, 2, E])
        chosen_sum = sb("chosen_sum", [P, 2, E], BF16)
        gap = sb("gap", [P, 2, 1])
        odds = sb("odds", [P, 2, 1])
        odds1 = sb("odds1", [P, 2, 1])
        share = sb("share", [P, 2, 1])
        base = sb("base", [P, E])
        place = sb("place", [P, 2, E])
        place2 = sb("place2", [P, 2, 2, E])
        place_f = sb("place_f", [P, 2, 2])
        place_i = sb("place_i", [P, 4, 2], I32)
        home = sb("home", [P, 2])

        bases = sb("bases", [P, E])
        pad_at = sb("pad_at", [P, E + 1])
        pad_i = sb("pad_i", [P, E + 1], I32)
        pad_rows = sb("pad_rows", [P, ROW])
        part = sb("part", [P, 1])
        fill = sb("fill", [P, E])
        marks = sb("marks", [P, T])
        over = sb("over", [P, E, T])
        blocks_of = sb("blocks_of", [P, E])
        ends = sb("ends", [P, E])
        ends_b = sb("ends_b", [P, E])
        blk_iota = sb("blk_iota", [P, BLOCKS])
        passed = sb("passed", [P, BLOCKS, E])
        passed_n = sb("passed_n", [P, BLOCKS, E])
        blk_e = sb("blk_e", [P, BLOCKS])
        blk_first = sb("blk_first", [P, BLOCKS])
        blk_live = sb("blk_live", [P, BLOCKS])
        blk_rel = sb("blk_rel", [P, BLOCKS])
        blk_row = sb("blk_row", [P, BLOCKS])
        blk_em = sb("blk_em", [P, BLOCKS])
        blk_e_i = sb("blk_e_i", [P, BLOCKS], I32)
        blk_row_i = sb("blk_row_i", [P, BLOCKS], I32)

        rows = sb("rows", [P, 8, ROW])
        rows_t = sb("rows_t", [P, 2, P])
        hid = sb("hid", [P, 2, 2 * H])
        silu = sb("silu", [P, 2, H])
        act_sb = sb("act_sb", [P, 2, H])
        act_t = sb("act_t", [P, 2, 2, P])
        y = sb("y_sb", [P, 2, D])
        yw = sb("yw", [P, 4, D])
        home_i = sb("home_i", [P, 4, 1], I32)

        CH = 4
        NC = T // CH
        res = sb("res", [P, 2, 2, CH, D])
        fin = sb("fin", [P, 2, CH, D])

        ps = ctx.enter_context(nc.psum_tensor("ps", [P, 8, 512], F32))
        score_ps = ps[:, 0:2, :]
        pt_ps = ps[:, 2:4, :]
        mix_ps = ps[:, 4, 0:256].rearrange("p (g q) -> p g q", g=2)
        val_ps = ps[:, 4, 256:384].rearrange("p (b j d) -> p b j d", b=2, d=HD)
        proj_ps = ps[:, 5, :]
        turn_ps = ps[:, 6, :]
        wo_ps = ps[:, 7, 0:128]
        gate_ps = ps[:, 7, 128:136]
        rank_ps = ps[:, 7, 136:152].rearrange("p (w e) -> p w e", w=2)
        back_ps = ps[:, 7, 256:512]

        w_in = sem("weights_in")
        w_in2 = sem("expert_weights_in")
        consts = sem("constants_made")
        p_set = sem("pool_setup_step")
        d_set = sem("dve_setup_step")
        setup = sem("setup_step")
        tanh_done = sem("tanh_done")
        bias_ps_done = sem("bias_product_done")
        setup_done = sem("setup_done")
        x_in = [sem(f"x_in{i}") for i in range(4)]
        c_in = [sem(f"ctx_in{i}") for i in range(4)]
        bn1 = sem("norm1_stats")
        agg1 = sem("norm1_aggregated")
        eps1 = sem("norm1_eps_added")
        pow1 = sem("norm1_rstd")
        xn_ready = sem("xn_ready")
        xb_ready = sem("x_plus_bias")
        turn_done = sem("turn_done")
        turned_ready = sem("turned_ready")
        proj_done = sem("proj_done")
        rope_muld = sem("rope_multiplied")
        rope_added = sem("rope_added")
        k_rot_ready = sem("k_rot_ready")
        k_bd_pool = sem("k_bd_by_pool")
        k_bd_act = sem("k_bd_by_act")
        q_bd_ready = sem("q_bd_ready")
        score_done = sem("score_done")
        peak_done = sem("peak_done")
        shifted = sem("scores_shifted")
        exp_done = sem("exp_done")
        pt_done = sem("probs_transposed")
        pt_ready = sem("probs_t_ready")
        mix_done = sem("values_and_mix_done")
        v_ready = sem("v_bd_ready")
        mixed_ready = sem("mixed_ready")
        back_done = sem("mix_turned_back")
        inv_done = sem("inverse_sum")
        o_ready = sem("o_ready")
        misc_done = sem("wo_gate_rank_done")
        x2_done = sem("x2_done")
        bn2 = sem("norm2_stats")
        agg2 = sem("norm2_aggregated")
        eps2 = sem("norm2_eps_added")
        pow2 = sem("norm2_rstd")
        xn2_ready = sem("xn2_ready")
        lg = sem("logits_ready")
        topd = sem("top_found")
        topi = sem("top_index_found")
        topf = sem("top_index_float")
        chose = sem("chosen_ready")
        chose_b = sem("chosen_sum_ready")
        gap_s = sem("gap_ready")
        odds_s = sem("odds_ready")
        odds1_s = sem("odds1_ready")
        share_s = sem("share_ready")
        w0_s = sem("first_weight_ready")
        w1_s = sem("second_weight_ready")
        place_s = sem("place_ready")
        base_s = sem("base_moved")
        place2_s = sem("place_masked")
        place_f_s = sem("place_summed")
        place_i_s = sem("place_index_ready")
        home_s = sem("home_written")
        home_m = sem("home_moved")
        scat = [sem(f"scattered{i}") for i in range(4)]
        pads = sem("pads_scattered")
        lst = sem("block_list_step")
        list_ready = sem("block_list_ready")
        pad_ready = sem("pad_ready")
        r_in = [sem(f"rows_in{i}") for i in range(8)]
        rt_done = sem("rows_turned")
        rt_ready = sem("rows_t_ready")
        h_done = sem("hidden_done")
        hb_done = sem("hidden_biased")
        silu_done = sem("silu_done")
        act_done = sem("act_done")
        at_done = sem("act_turned")
        at_ready = sem("act_t_ready")
        y_done = sem("y_done")
        yb_done = sem("y_biased")
        yw_done = sem("y_weighted")
        home_done = sem("home_index_ready")
        y_out = [sem(f"y_scattered{i}") for i in range(4)]
        res_in = [sem(f"results_in{i}") for i in range(2)]
        both = sem("both_experts_added")
        fin_done = sem("final_sum")
        stored = [sem(f"stored{i}") for i in range(2)]

        W_LOADS = 15
        program = ctx.enter_context(nc.Block())

        def wide(src, n):
            return src.rearrange("(a n) -> a n", a=1).to_broadcast([n, src.shape[0]])

        xd = a["x"].rearrange("b s d -> (b s) d")
        cd = a["ctx_1024"].rearrange("b s d -> (b s) d")
        od = out.rearrange("b s d -> (b s) d").rearrange("(t p) d -> p t d", p=P)

        def counted(engine, value):
            value = value if isinstance(value, int) else engine.to_reg(value)
            engine.wait_ge(setup_done, 1)
            return value

        @program.sync
        def _(sp):
            sp.dma_start(wk[:], a["wk"]).then_inc(w_in, 16)
            sp.dma_start(wq[:], a["wq"]).then_inc(w_in, 16)
            sp.dma_start(wv[:], a["wv"]).then_inc(w_in, 16)
            sp.dma_start(wo[:], a["wo"]).then_inc(w_in, 16)
            sp.dma_start(turn_tab[:], a["turn"]).then_inc(w_in, 16)
            for b in range(2):
                sp.dma_start(qb_col[64 * b:64 * b + 64], a["qb"]).then_inc(w_in, 16)
                sp.dma_start(kb_col[64 * b:64 * b + 64], a["kb"]).then_inc(w_in, 16)
            sp.dma_start(bv_col[:], a["L0_xattn_bv"].rearrange("(d a) -> d a", a=1)).then_inc(w_in, 16)
            sp.dma_start(bo_wide[:], wide(a["L0_xattn_bo"], P)).then_inc(w_in, 16)
            sp.dma_start(gates[:, 0:1], wide(a["g_xattn"], P)).then_inc(w_in, 16)
            sp.dma_start(gates[:, 1:2], wide(a["g_ffn"], P)).then_inc(w_in, 16)
            sp.dma_start(gate_w[:], a["gate_w"]).then_inc(w_in, 16)
            sp.dma_start(gate_b[:], wide(a["L0_ffn_gate_b"], P)).then_inc(w_in, 16)

            def load(ii, k):
                if runs(ii, k, NORM1):
                    t = tile(ii, k, NORM1)
                    if runs(ii, k, NORM1 + 4):
                        sp.wait_ge(bn1, t - 3)
                        sp.wait_ge(turn_done, t - 3)
                    sp.dma_start(x[:, t, :], xd[bass.ts(t, P), :]).then_inc(x_in[k % 4], 16)
                    sp.dma_start(ctx_in[:, k % 4, :], cd[bass.ts(t, P), :]).then_inc(c_in[k % 4], 16)

            for k in range(4):
                load(0, k)
            sp.dma_start(w01[:], a["w01"]).then_inc(w_in2, 16)
            sp.dma_start(w2[:], a["w2"]).then_inc(w_in2, 16)
            sp.dma_start(b01[:], wide(a["b01"], P)).then_inc(w_in2, 16)
            sp.dma_start(b2[:], wide(a["b2"], P)).then_inc(w_in2, 16)
            with sp.Fori(1, T // 4) as ii:
                for k in range(4):
                    load(ii, k)

            sp.wait_ge(list_ready, 1)
            for q in scat:
                sp.wait_ge(q, 32 * T // 4)
            sp.wait_ge(pads, 16 * (E + 1))

            def load_block(lap, k, again):
                if again:
                    sp.wait_ge(yb_done, 8 * lap + k - 7)
                    sp.wait_ge(yw_done, 8 * lap + k - 7)
                    sp.wait_ge(home_done, 8 * lap + k - 7)
                at = sp.value_load(blk_row_i[0:1, bass.ds(8 * lap + k, 1)], min_val=0, max_val=E * REGION)
                sp.dma_start(rows[:, k, :], rows_dram[bass.ds(at, P), :]).then_inc(r_in[k], 16)

            for k in range(8):
                load_block(0, k, False)
            with sp.Fori(1, BLOCKS // 8) as lap:
                for k in range(8):
                    load_block(lap, k, True)

            for q in y_out:
                sp.wait_ge(q, 16 * BLOCKS // 4)
            rd = result_dram.rearrange("(s t p) d -> p s t d", s=2, p=P)

            def chunk(lap, k, again):
                c = 2 * lap + k
                if again:
                    sp.wait_ge(fin_done, c - 1)
                for slot in range(2):
                    sp.dma_start(res[:, k, slot], rd[:, slot, bass.ds(CH * c, CH), :]).then_inc(res_in[k], 16)

            def store(lap, k):
                c = 2 * lap + k
                sp.wait_ge(fin_done, c + 1)
                sp.dma_start(od[:, bass.ds(CH * c, CH), :], fin[:, k]).then_inc(stored[k], 16)

            for k in range(2):
                chunk(0, k, False)
            with sp.Fori(1, NC // 2) as lap:
                for k in range(2):
                    chunk(lap, k, True)
                    store(lap - 1, k)
            for k in range(2):
                store(NC // 2 - 1, k)
            for k in range(2):
                sp.wait_ge(stored[k], 16 * (NC // 2))

        @program.tensor
        def _(pe):
            pe.wait_ge(setup, 1)
            nc.tensor.matmul(wo_ps, bv_wide[:], wo[:], start=True, stop=True).then_inc(bias_ps_done, 1)
            pe.wait_ge(consts, 2)
            pe.wait_ge(setup_done, 1)

            def step(ii, k):
                s = 4 * ii + k
                if runs(ii, k, PROB):
                    t = tile(ii, k, PROB)
                    r = (k - PROB) % 2
                    for u in range(2):
                        pe.wait_ge(exp_done, 2 * t + u + 1)
                        if runs(ii, k, PROB + 1):
                            pe.wait_ge(pt_ready, 2 * t + u - 1)
                        for j in range(4):
                            last = nc.tensor.transpose(
                                pt_ps[:, u, j * P:(j + 1) * P],
                                probs[:, r, u, 2 * j:2 * j + 2, :].rearrange("p h k -> p (h k)"), ident[:])
                        last.then_inc(pt_done, 1)
                if runs(ii, k, SCORE):
                    t = tile(ii, k, SCORE)
                    n = (k - SCORE) % 4 // 2
                    h = k % 2
                    unit = 2 * ii + (k - SCORE) // 2
                    pe.wait_ge(q_bd_ready, 2 * unit + 2)
                    pe.wait_ge(k_bd_pool, unit + 1)
                    pe.wait_ge(k_bd_act, unit + 1)
                    for u in range(2):
                        if runs(ii, k, SCORE + 1):
                            pe.wait_ge(shifted, 2 * t + u - 1)
                        nc.tensor.matmul(score_ps[:, u, :],
                                         q_bd[:, n, h, u].rearrange("p b q -> p (b q)"),
                                         k_bd[:, n, h, u].rearrange("p h k -> p (h k)"),
                                         start=True, stop=True).then_inc(score_done, 1)
                if not isinstance(ii, int) or 1 <= s < T + GATE:
                    if not isinstance(ii, int) or s > 1:
                        pe.wait_ge(turned_ready, s - 1)
                    if runs(ii, k, TURN):
                        t = tile(ii, k, TURN)
                        r = (k - TURN) % 4
                        pe.wait_ge(xn_ready, t + 1)
                        last = nc.tensor.transpose(turn_ps[:, 0:128], xn[:, r % 2, :], ident[:])
                        pe.wait_ge(c_in[r], 16 * (ii + (k - TURN) // 4 + 1))
                        last = nc.tensor.transpose(turn_ps[:, 128:256], ctx_in[:, r, :], ident[:])
                    if runs(ii, k, WO):
                        pe.wait_ge(o_ready, tile(ii, k, WO) + 1)
                        last = nc.tensor.transpose(turn_ps[:, 256:384], o[:, (k - WO) % 2, :], ident[:])
                    if runs(ii, k, GATE):
                        pe.wait_ge(xn2_ready, tile(ii, k, GATE) + 1)
                        last = nc.tensor.transpose(turn_ps[:, 384:512], routed[:, (k - GATE) % 4, 0, 0:D], ident[:])
                    last.then_inc(turn_done, 1)
                if runs(ii, k, VALUE) or runs(ii, k, PROB):
                    if runs(ii, k, VALUE + 1):
                        pe.wait_ge(v_ready, tile(ii, k, VALUE))
                    if runs(ii, k, PROB + 1):
                        pe.wait_ge(mixed_ready, tile(ii, k, PROB))
                    if runs(ii, k, VALUE):
                        pe.wait_ge(turned_ready, s - 1)
                        for b in range(2):
                            for h in range(2):
                                last = nc.tensor.matmul(
                                    val_ps[64 * h:64 * h + 64, b].rearrange("p j d -> p (j d)"),
                                    turned[:, (k - VALUE) % 4, 1, 64 * b:64 * b + 64],
                                    wv[:, 64 * h:64 * h + 64], start=True, stop=True)
                    if runs(ii, k, PROB):
                        t = tile(ii, k, PROB)
                        pe.wait_ge(v_ready, t + 1)
                        for g in range(2):
                            pe.wait_ge(pt_ready, 2 * t + g + 1)
                            for b in range(2):
                                for j in range(4):
                                    last = nc.tensor.matmul(
                                        mix_ps[32 * j:32 * j + 32, g, 64 * b:64 * b + 64],
                                        v_bd[:, (k - PROB) % 4, b, 4 * g + j, :],
                                        probs_t[:, (k - PROB) % 2, 4 * g + j, 64 * b:64 * b + 64],
                                        start=True, stop=True)
                    last.then_inc(mix_done, 1)
                if runs(ii, k, WO) or runs(ii, k, GATE) or runs(ii, k, ROUTE):
                    if runs(ii, k, WO) or runs(ii, k, GATE):
                        pe.wait_ge(turned_ready, s)
                    if runs(ii, k, WO):
                        pe.wait_ge(o_ready, tile(ii, k, WO) + 1)
                    if isinstance(ii, int):
                        for done, lag in ((x2_done, WO), (lg, GATE), (place_s, ROUTE), (base_s, ROUTE)):
                            if runs(ii, k, lag + 1):
                                pe.wait_ge(done, tile(ii, k, lag))
                    if runs(ii, k, WO):
                        last = nc.tensor.matmul(wo_ps, turned[:, (k - TURN) % 4, 2, :], wo_gated[:],
                                                start=True, stop=True)
                    if runs(ii, k, GATE):
                        last = nc.tensor.matmul(gate_ps, turned[:, (k - TURN) % 4, 3, :], gate_w[:],
                                                start=True, stop=True)
                    if runs(ii, k, ROUTE):
                        pe.wait_ge(chose_b, tile(ii, k, ROUTE) + 1)
                        for w in range(2):
                            last = nc.tensor.matmul(rank_ps[:, w, :], before[:, w, :],
                                                    chosen_sum[:, (k - ROUTE) % 2, :], start=True, stop=True)
                    last.then_inc(misc_done, 1)
                even = k % 2 == 0
                lag = 2 if even else 3
                if runs(ii, k, lag):
                    w, src = (wk, 1) if even else (wq, 0)
                    r = (k - lag) % 4
                    if not isinstance(ii, int) or s > 2:
                        pe.wait_ge(rope_muld, s - 2)
                    pe.wait_ge(turned_ready, s)
                    for turn in range(2):
                        for u in range(2):
                            for b in range(2):
                                last = nc.tensor.matmul(
                                    proj_ps[64 * b:64 * b + 64, 256 * turn + 128 * u:256 * turn + 128 * u + 128],
                                    w[:, turn, 64 * u:64 * u + 64],
                                    turned[:, r:r + 2, src, 64 * b:64 * b + 64],
                                    start=True, stop=True)
                    last.then_inc(proj_done, 1)
                if runs(ii, k, PROB):
                    pe.wait_ge(mixed_ready, tile(ii, k, PROB) + 1)
                    for done, lag in ((x2_done, WO), (lg, GATE), (place_s, ROUTE), (base_s, ROUTE)):
                        if runs(ii, k, lag):
                            pe.wait_ge(done, tile(ii, k, lag) + 1)
                    for g in range(2):
                        last = nc.tensor.transpose(back_ps[:, g * P:(g + 1) * P], mixed[:, (k - PROB) % 2, g, :], ident[:])
                    last.then_inc(back_done, 1)

            steps(pe, step)

            pe.wait_ge(w_in2, 64)
            pe.wait_ge(list_ready, 1)

            def block_step(ii, k):
                if block_runs(ii, k, HIDDEN):
                    j = block(ii, k, HIDDEN)
                    r = (k - HIDDEN) % 2
                    e = pe.value_load(blk_e_i[0:1, bass.ds(j, 1)], min_val=0, max_val=E - 1)
                    pe.wait_ge(rt_ready, j + 1)
                    if block_runs(ii, k, HIDDEN + 2):
                        pe.wait_ge(hb_done, j - 1)
                    nc.tensor.matmul(ps[:, r, :], rows_t[:, r, :], w01[:, bass.ds(e * (2 * H), 2 * H)],
                                     start=True, stop=True).then_inc(h_done, 1)
                if block_runs(ii, k, ROWS_T):
                    j = block(ii, k, ROWS_T)
                    pe.wait_ge(r_in[k], 16 * ii + 16)
                    if block_runs(ii, k, ROWS_T + 2):
                        pe.wait_ge(rt_ready, j - 1)
                    nc.tensor.transpose(ps[:, 2 + k % 2, 0:P], rows[:, k, 0:D], ident[:]).then_inc(rt_done, 1)
                if block_runs(ii, k, ACT_T):
                    j = block(ii, k, ACT_T)
                    r = (k - ACT_T) % 2
                    pe.wait_ge(act_done, j + 1)
                    if block_runs(ii, k, ACT_T + 2):
                        pe.wait_ge(at_ready, j - 1)
                    for c in range(2):
                        last = nc.tensor.transpose(ps[:, 4 + r, c * P:(c + 1) * P],
                                                   act_sb[:, r, c * P:(c + 1) * P], ident[:])
                    last.then_inc(at_done, 1)
                if block_runs(ii, k, RESULT):
                    j = block(ii, k, RESULT)
                    r = (k - RESULT) % 2
                    e = pe.value_load(blk_e_i[0:1, bass.ds(j, 1)], min_val=0, max_val=E - 1)
                    pe.wait_ge(at_ready, j + 1)
                    if block_runs(ii, k, RESULT + 2):
                        pe.wait_ge(yb_done, j - 1)
                    for c in range(2):
                        last = nc.tensor.matmul(ps[:, 6 + r, 0:D], act_t[:, r, c, :],
                                                w2[:, bass.ds(e * (2 * D) + c * D, D)], start=(c == 0), stop=(c == 1))
                    last.then_inc(y_done, 1)

            block_steps(pe, block_step)

        @program.scalar
        def _(act):
            act.wait_ge(w_in, 16 * W_LOADS)
            nc.scalar.activation(tgate[:], gates[:], ACT.Tanh).then_inc(tanh_done, 1)
            act.wait_ge(consts, 2)
            act.wait_ge(setup_done, 1)

            def step(ii, k):
                s = 4 * ii + k
                if runs(ii, k, PROB):
                    t = tile(ii, k, PROB)
                    for u in range(2):
                        act.wait_ge(pt_done, 2 * t + u + 1)
                        nc.scalar.copy(probs_t[:, (k - PROB) % 2, 4 * u:4 * u + 4, :].rearrange("p j q -> p (j q)"),
                                       pt_ps[:, u, :]).then_inc(pt_ready, 1)

                def exponentials(u):
                    if runs(ii, k, SCORE):
                        t = tile(ii, k, SCORE)
                        v = probs[:, k % 2, u].rearrange("p h k -> p (h k)")
                        act.wait_ge(shifted, 2 * t + u + 1)
                        nc.scalar.activation(v, v, ACT.Exp, scale=SCALE).then_inc(exp_done, 1)

                exponentials(0)
                if not isinstance(ii, int) or 1 <= s < T + GATE:
                    act.wait_ge(turn_done, s)
                    nc.scalar.copy(turned[:, (k - TURN) % 4].rearrange("p w t -> p (w t)"),
                                   turn_ps).then_inc(turned_ready, 1)
                exponentials(1)
                if runs(ii, k, ROUTE):
                    t = tile(ii, k, ROUTE)
                    r = (k - ROUTE) % 2
                    act.wait_ge(gap_s, t + 1)
                    nc.scalar.activation(odds[:, r, :], gap[:, r, :], ACT.Exp).then_inc(odds_s, 1)
                if runs(ii, k, VALUE) or runs(ii, k, PROB):
                    act.wait_ge(mix_done, s - VALUE + 1)
                    if runs(ii, k, VALUE):
                        for h in range(2):
                            last = nc.scalar.copy(
                                v_bd[64 * h:64 * h + 64, (k - VALUE) % 4, :, :, 9 * h:9 * h + HD],
                                val_ps[64 * h:64 * h + 64])
                        last.then_inc(v_ready, 1)
                    if runs(ii, k, PROB):
                        nc.scalar.copy(mixed[:, (k - PROB) % 2], mix_ps).then_inc(mixed_ready, 1)
                if k % 2 and runs(ii, k, 3):
                    n = 2 * ii + (k - 3) // 2
                    act.wait_ge(k_rot_ready, n + 1)
                    if runs(ii, k, 7):
                        act.wait_ge(score_done, 4 * n - 4)
                    for h in range(4, 8):
                        last = nc.scalar.activation(k_bd[:, (k - 3) // 2 % 2, :, :, h, :],
                                                    k_rot.rearrange("p u t k -> p t u k"), ACT.Copy,
                                                    scale=head_mask[:, h:h + 1])
                    last.then_inc(k_bd_act, 1)

            steps(act, step)

            def block_step(ii, k):
                if block_runs(ii, k, ROWS_T):
                    j = block(ii, k, ROWS_T)
                    act.wait_ge(rt_done, j + 1)
                    nc.scalar.copy(rows_t[:, k % 2, :], ps[:, 2 + k % 2, 0:P]).then_inc(rt_ready, 1)
                if block_runs(ii, k, ACT_T):
                    j = block(ii, k, ACT_T)
                    r = (k - ACT_T) % 2
                    act.wait_ge(at_done, j + 1)
                    nc.scalar.copy(act_t[:, r].rearrange("p c t -> p (c t)"),
                                   ps[:, 4 + r, 0:2 * P]).then_inc(at_ready, 1)
                if block_runs(ii, k, HIDDEN):
                    j = block(ii, k, HIDDEN)
                    r = (k - HIDDEN) % 2
                    act.wait_ge(hb_done, j + 1)
                    if block_runs(ii, k, HIDDEN + 2):
                        act.wait_ge(act_done, j - 1)
                    nc.scalar.activation(silu[:, r, :], hid[:, r, H:2 * H], ACT.Silu).then_inc(silu_done, 1)
                if block_runs(ii, k, RESULT):
                    j = block(ii, k, RESULT)
                    act.wait_ge(yb_done, j + 1)
                    if block_runs(ii, k, RESULT + 4):
                        act.wait_ge(y_out[(k - RESULT) % 4], 16 * (2 * ii + (k - RESULT) // 4))
                    nc.scalar.activation(yw[:, (k - RESULT) % 4, :], y[:, (k - RESULT) % 2, :], ACT.Copy,
                                         scale=rows[:, (k - RESULT) % 8, D:D + 1]).then_inc(yw_done, 1)

            block_steps(act, block_step)

        @program.gpsimd
        def _(pool):
            nc.gpsimd.memset(ident[:], 0.0).then_inc(p_set, 1)
            nc.gpsimd.memset(before[:], 1.0).then_inc(p_set, 1)
            nc.gpsimd.memset(mask_by_b[:], 1.0).then_inc(p_set, 1)
            nc.gpsimd.memset(half[:], -0.5).then_inc(p_set, 1)
            pool.wait_ge(p_set, 4)
            nc.gpsimd.affine_select(out=ident[:], in_=ident[:], compare_op=ALU.not_equal, fill=1.0, base=0,
                                    pattern=[[-1, P]], channel_multiplier=1).then_inc(consts, 1)
            nc.gpsimd.affine_select(out=before[:, 0, :], in_=before[:, 0, :], compare_op=ALU.is_gt, fill=0.0, base=0,
                                    pattern=[[1, P]], channel_multiplier=-1).then_inc(consts, 1)
            nc.gpsimd.affine_select(out=mask_by_b[:], in_=mask_by_b[:], compare_op=ALU.is_ge, fill=0.0, base=0,
                                    pattern=[[-64, 2], [-HD, 8]], channel_multiplier=1).then_inc(p_set, 1)
            pool.wait_ge(p_set, 5)
            nc.gpsimd.affine_select(out=mask_by_b[:], in_=mask_by_b[:], compare_op=ALU.is_ge, fill=0.0, base=HD - 1,
                                    pattern=[[64, 2], [HD, 8]], channel_multiplier=-1).then_inc(p_set, 1)
            nc.gpsimd.iota(iota8[:], [[0, 2], [1, E]], base=0, channel_multiplier=0,
                           allow_small_or_imprecise_dtypes=True).then_inc(p_set, 1)
            nc.gpsimd.iota(home[:], [[TOKENS, 2]], base=0, channel_multiplier=1,
                           allow_small_or_imprecise_dtypes=True).then_inc(p_set, 1)
            nc.gpsimd.iota(bases[:], [[REGION, E]], base=0, channel_multiplier=0,
                           allow_small_or_imprecise_dtypes=True).then_inc(p_set, 1)
            nc.gpsimd.iota(marks[:], [[P, T]], base=0, channel_multiplier=0,
                           allow_small_or_imprecise_dtypes=True).then_inc(p_set, 1)
            nc.gpsimd.iota(blk_iota[:], [[1, BLOCKS]], base=0, channel_multiplier=0,
                           allow_small_or_imprecise_dtypes=True).then_inc(p_set, 1)
            nc.gpsimd.iota(part[:], [[0, 1]], base=0, channel_multiplier=1,
                           allow_small_or_imprecise_dtypes=True).then_inc(p_set, 1)
            nc.gpsimd.memset(k_bd[:], 0.0).then_inc(p_set, 1)
            pool.wait_ge(setup_done, 1)

            def scatter(ii, k):
                t = tile(ii, k, SCATTER)
                r = (k - SCATTER) % 4
                due = counted(pool, t + 1)
                pool.wait_ge(place_i_s, due)
                pool.wait_ge(home_s, due)
                pool.wait_ge(w1_s, due)
                for slot in range(2):
                    nc.gpsimd.indirect_dma_start(
                        out=rows_dram, out_offset=bass.IndirectOffsetOnAxis(ap=place_i[:, r, slot:slot + 1], axis=0),
                        in_=routed[:, r, slot, :], in_offset=None).then_inc(scat[r], 16)

            def power(mv, rstd, k, t, agg, eps, done):
                due = counted(pool, t + 1)
                pool.wait_ge(agg, due)
                nc.gpsimd.tensor_scalar(rstd[:, k, 0:1], mv[:, k, 1:2], EPS, None, ALU.add).then_inc(eps, 1)
                pool.wait_ge(eps, t + 1)
                nc.gpsimd.tensor_tensor(rstd[:, k, 1:2], rstd[:, k, 0:1], half[:], ALU.pow).then_inc(done, 1)

            def step(ii, k):
                if k % 2 and runs(ii, k, 3):
                    n = 2 * ii + (k - 3) // 2
                    pool.wait_ge(k_rot_ready, n + 1)
                    if runs(ii, k, 7):
                        due = counted(pool, 4 * n - 4)
                        pool.wait_ge(score_done, due)
                    for h in range(4):
                        last = nc.gpsimd.tensor_scalar(k_bd[:, (k - 3) // 2 % 2, :, :, h, :],
                                                       k_rot.rearrange("p u t k -> p t u k"), head_mask[:, h:h + 1],
                                                       None, ALU.mult)
                    last.then_inc(k_bd_pool, 1)
                if runs(ii, k, SCATTER):
                    scatter(ii, k)
                if runs(ii, k, NORM1):
                    power(mv1, rstd1, k % 4, tile(ii, k, NORM1), agg1, eps1, pow1)
                if runs(ii, k, 1):
                    t = tile(ii, k, 1)
                    pool.wait_ge(xn_ready, t + 1)
                    nc.gpsimd.tensor_tensor(x[:, t, :], x[:, t, :], bo_wide[:], ALU.add).then_inc(xb_ready, 1)
                if runs(ii, k, WO):
                    power(mv2, rstd2, (k - WO) % 4, tile(ii, k, WO), agg2, eps2, pow2)

            steps(pool, step)

            pool.wait_ge(pad_ready, 1)
            for e in range(E + 1):
                pool.wait_ge(setup_done, 1)
                nc.gpsimd.indirect_dma_start(
                    out=rows_dram, out_offset=bass.IndirectOffsetOnAxis(ap=pad_i[:, e:e + 1], axis=0),
                    in_=pad_rows[:], in_offset=None).then_inc(pads, 16)

            def block_step(ii, k):
                if block_runs(ii, k, RESULT):
                    j = block(ii, k, RESULT)
                    r = (k - RESULT) % 4
                    due = counted(pool, j + 1)
                    pool.wait_ge(yw_done, due)
                    pool.wait_ge(home_done, due)
                    nc.gpsimd.indirect_dma_start(
                        out=result_dram, out_offset=bass.IndirectOffsetOnAxis(ap=home_i[:, r, :], axis=0),
                        in_=yw[:, r, :], in_offset=None, bounds_check=2 * TOKENS - 1,
                        oob_is_err=False).then_inc(y_out[r], 16)

            block_steps(pool, block_step)

            def finish(lap, k, again):
                c = 2 * lap + k
                pool.wait_ge(both, c + 1)
                if again:
                    pool.wait_ge(stored[k], 16 * lap)
                nc.gpsimd.tensor_tensor(fin[:, k], res[:, k, 0], x[:, bass.ds(CH * c, CH), :], ALU.add).then_inc(fin_done, 1)

            for k in range(2):
                finish(0, k, False)
            with pool.Fori(1, NC // 2) as lap:
                for k in range(2):
                    finish(lap, k, True)

        @program.vector
        def _(dve):
            nc.vector.memset(q_bd[:], 0.0).then_inc(d_set, 1)
            nc.vector.memset(v_bd[:], 0.0).then_inc(d_set, 1)
            nc.vector.memset(turn_ps, 0.0).then_inc(d_set, 1)
            nc.vector.memset(pad_rows[:], 0.0).then_inc(d_set, 1)
            nc.vector.memset(bv_wide[:], 1.0).then_inc(d_set, 1)
            dve.wait_ge(d_set, 5)
            nc.vector.memset(v_bd[0:64, :, :, :, HD:HD + 1], 1.0).then_inc(d_set, 1)
            nc.vector.memset(v_bd[64:128, :, :, :, 2 * HD + 1:2 * HD + 2], 1.0).then_inc(d_set, 1)
            nc.vector.memset(pad_rows[:, D + 1:D + 2], float(NOWHERE)).then_inc(d_set, 1)
            dve.wait_ge(w_in, 16 * W_LOADS)
            nc.vector.tensor_scalar(bv_wide[:], bv_wide[:], bv_col[:], None, ALU.mult).then_inc(setup, 1)
            dve.wait_ge(tanh_done, 1)
            nc.vector.tensor_scalar(wo_gated[:], wo[:], tgate[:, 0:1], None, ALU.mult).then_inc(d_set, 1)
            dve.wait_ge(bias_ps_done, 1)
            nc.vector.tensor_tensor(bo_wide[:], wo_ps, bo_wide[:], ALU.add).then_inc(d_set, 1)
            dve.wait_ge(d_set, 10)
            nc.vector.tensor_scalar(bo_wide[:], bo_wide[:], tgate[:, 0:1], None, ALU.mult).then_inc(d_set, 1)
            done = 11
            for col, tab in ((qb_col, qb_tab), (kb_col, kb_tab)):
                for u in range(2):
                    nc.vector.tensor_scalar(bt_tmp[:, u, :], turn_tab[:, 0, :], col[:, 0, u:u + 1],
                                            None, ALU.mult).then_inc(d_set, 1)
                    nc.vector.tensor_scalar(tab[:, u, 0, :], turn_tab[:, 1, :], col[:, 1, u:u + 1],
                                            None, ALU.mult).then_inc(d_set, 1)
                done += 4
                dve.wait_ge(d_set, done)
                nc.vector.tensor_tensor(tab[:, :, 1, :], tab[:, :, 0, :], bt_tmp[:], ALU.add).then_inc(d_set, 1)
                dve.wait_ge(d_set, done + 1)
                nc.vector.tensor_copy(tab[:, :, 0, :], tab[:, :, 1, :]).then_inc(d_set, 1)
                done += 2
                dve.wait_ge(d_set, done)
            dve.wait_ge(p_set, 13)
            nc.vector.tensor_tensor(head_mask[:], mask_by_b[:, 0], mask_by_b[:, 1], ALU.add).then_inc(d_set, 1)
            dve.wait_ge(d_set, done + 1)
            nc.vector.tensor_copy(base[:], bases[:]).then_inc(setup_done, 1)
            dve.wait_ge(setup_done, 1)

            def step(ii, k):
                s = 4 * ii + k
                if runs(ii, k, GATE):
                    t = tile(ii, k, GATE)
                    r = (k - GATE) % 4
                    dve.wait_ge(pow2, t + 1)
                    if runs(ii, k, GATE + 4):
                        dve.wait_ge(scat[r], 32 * (ii + (k - GATE) // 4))
                    nc.vector.tensor_scalar(routed[:, r, :, 0:D], x[:, t, :].unsqueeze(1).to_broadcast([P, 2, D]),
                                            mv2[:, r, 0:1], rstd2[:, r, 1:2], ALU.subtract, ALU.mult).then_inc(xn2_ready, 1)
                if runs(ii, k, SCORE):
                    t = tile(ii, k, SCORE)
                    r = k % 2
                    for u in range(2):
                        v = score_ps[:, u, :].rearrange("p (h k) -> p h k", h=8)
                        m = peak[:, r, 8 * u:8 * u + 8]
                        dve.wait_ge(score_done, 2 * t + u + 1)
                        nc.vector.tensor_reduce(m, v, AX.X, ALU.max).then_inc(peak_done, 1)
                        dve.wait_ge(peak_done, 2 * t + u + 1)
                        nc.vector.tensor_tensor(probs[:, r, u], v, m.unsqueeze(2).to_broadcast([P, 8, S]),
                                                ALU.subtract).then_inc(shifted, 1)
                if runs(ii, k, NORM1):
                    t = tile(ii, k, NORM1)
                    due = counted(dve, 16 * (ii + k // 4 + 1))
                    dve.wait_ge(x_in[k % 4], due)
                    nc.vector.bn_stats(stats1[:, k % 4, :], x[:, t, :]).then_inc(bn1, 1)
                    due = counted(dve, t + 1)
                    dve.wait_ge(bn1, due)
                    nc.vector.bn_aggr(mv1[:, k % 4, :], stats1[:, k % 4, :]).then_inc(agg1, 1)
                if runs(ii, k, ROUTE):
                    t = tile(ii, k, ROUTE)
                    r = (k - ROUTE) % 2
                    due = counted(dve, t + 1)
                    dve.wait_ge(lg, due)
                    nc.vector.max(top[:, r, :], logits[:, r, :]).then_inc(topd, 1)
                    due = counted(dve, t + 1)
                    dve.wait_ge(topd, due)
                    nc.vector.max_index(top_at[:, r, :], top[:, r, :], logits[:, r, :]).then_inc(topi, 1)
                    nc.vector.tensor_tensor(gap[:, r, :], top[:, r, 1:2], top[:, r, 0:1], ALU.subtract).then_inc(gap_s, 1)
                    dve.wait_ge(topi, t + 1)
                    nc.vector.tensor_copy(top_f[:, r, :], top_at[:, r, 0:2]).then_inc(topf, 1)
                    dve.wait_ge(topf, t + 1)
                    nc.vector.tensor_tensor(chosen[:, r], iota8[:], top_f[:, r, :].unsqueeze(2).to_broadcast([P, 2, E]),
                                            ALU.is_equal).then_inc(chose, 1)
                    dve.wait_ge(chose, t + 1)
                    nc.vector.tensor_tensor(chosen_sum[:, r, :], chosen[:, r, 0], chosen[:, r, 1], ALU.add).then_inc(chose_b, 1)
                if runs(ii, k, NORM1):
                    t = tile(ii, k, NORM1)
                    dve.wait_ge(pow1, t + 1)
                    if runs(ii, k, NORM1 + 2):
                        dve.wait_ge(turn_done, s - 1)
                    nc.vector.tensor_scalar(xn[:, k % 2, :], x[:, t, :], mv1[:, k % 4, 0:1], rstd1[:, k % 4, 1:2],
                                            ALU.subtract, ALU.mult).then_inc(xn_ready, 1)
                if runs(ii, k, WO) or runs(ii, k, GATE) or runs(ii, k, ROUTE):
                    dve.wait_ge(misc_done, s - WO + 1)
                if runs(ii, k, WO):
                    t = tile(ii, k, WO)
                    dve.wait_ge(xb_ready, t + 1)
                    nc.vector.tensor_tensor(x[:, t, :], wo_ps, x[:, t, :], ALU.add).then_inc(x2_done, 1)
                if runs(ii, k, GATE):
                    nc.vector.tensor_tensor(logits[:, (k - GATE) % 2, :], gate_ps, gate_b[:], ALU.add).then_inc(lg, 1)
                if runs(ii, k, ROUTE):
                    t = tile(ii, k, ROUTE)
                    r = (k - ROUTE) % 2
                    nc.vector.tensor_tensor(place[:, r, :], rank_ps[:, 0, :], base[:], ALU.add).then_inc(place_s, 1)
                    nc.vector.tensor_tensor(base[:], rank_ps[:, 1, :], base[:], ALU.add).then_inc(base_s, 1)
                if runs(ii, k, WO):
                    t = tile(ii, k, WO)
                    r = (k - WO) % 4
                    due = counted(dve, t + 1)
                    dve.wait_ge(x2_done, due)
                    nc.vector.bn_stats(stats2[:, r, :], x[:, t, :]).then_inc(bn2, 1)
                    due = counted(dve, t + 1)
                    dve.wait_ge(bn2, due)
                    nc.vector.bn_aggr(mv2[:, r, :], stats2[:, r, :]).then_inc(agg2, 1)
                if runs(ii, k, ROUTE):
                    t = tile(ii, k, ROUTE)
                    r = (k - ROUTE) % 2
                    q = (k - ROUTE) % 4
                    dve.wait_ge(place_s, t + 1)
                    nc.vector.tensor_tensor(place2[:, r], chosen[:, r], place[:, r, :].unsqueeze(1).to_broadcast([P, 2, E]),
                                            ALU.mult).then_inc(place2_s, 1)
                    dve.wait_ge(odds_s, t + 1)
                    nc.vector.tensor_scalar(odds1[:, r, :], odds[:, r, :], 1.0, None, ALU.add).then_inc(odds1_s, 1)
                    dve.wait_ge(place2_s, t + 1)
                    nc.vector.tensor_reduce(place_f[:, r, :], place2[:, r], AX.X, ALU.add).then_inc(place_f_s, 1)
                    dve.wait_ge(odds1_s, t + 1)
                    nc.vector.reciprocal(share[:, r, :], odds1[:, r, :]).then_inc(share_s, 1)
                    dve.wait_ge(place_f_s, t + 1)
                    nc.vector.tensor_copy(place_i[:, q, :], place_f[:, r, :]).then_inc(place_i_s, 1)
                    if not isinstance(ii, int) or t > 0:
                        dve.wait_ge(home_m, t)
                    nc.vector.tensor_copy(routed[:, q, :, D + 1], home[:]).then_inc(home_s, 1)
                    dve.wait_ge(share_s, t + 1)
                    nc.vector.tensor_tensor(routed[:, q, 0, D:D + 1], share[:, r, :], tgate[:, 1:2], ALU.mult).then_inc(w0_s, 1)
                    dve.wait_ge(home_s, t + 1)
                    nc.vector.tensor_scalar(home[:], home[:], float(P), None, ALU.add).then_inc(home_m, 1)
                    dve.wait_ge(w0_s, t + 1)
                    nc.vector.tensor_tensor(routed[:, q, 1, D:D + 1], routed[:, q, 0, D:D + 1], odds[:, r, :],
                                            ALU.mult).then_inc(w1_s, 1)
                lag = 2 if k % 2 == 0 else 3
                if runs(ii, k, lag):
                    n = 2 * ii + (k - lag) // 2
                    dve.wait_ge(proj_done, s - 1)
                    nc.vector.tensor_tensor(
                        rope_mul[:].rearrange("p w u t k -> p w (u t) k"),
                        proj_ps.rearrange("p (w c k) -> p w c k", w=2, k=S),
                        turn_tab[:].unsqueeze(2).to_broadcast([P, 2, 4, S]), ALU.mult).then_inc(rope_muld, 1)
                    dve.wait_ge(rope_muld, s - 1)
                    nc.vector.tensor_tensor(rope_sum[:], rope_mul[:, 0], rope_mul[:, 1], ALU.add).then_inc(rope_added, 1)
                    dve.wait_ge(rope_added, s - 1)
                    if k % 2 == 0:
                        if runs(ii, k, 4):
                            dve.wait_ge(k_bd_pool, n)
                            dve.wait_ge(k_bd_act, n)
                        nc.vector.tensor_tensor(k_rot, rope_sum[:], kb_tab[:], ALU.add).then_inc(k_rot_ready, 1)
                    else:
                        if runs(ii, k, 7):
                            dve.wait_ge(score_done, 4 * n - 4)
                        for b in range(2):
                            rows_b = slice(64 * b, 64 * b + 64)
                            nc.vector.tensor_tensor(
                                q_bd[rows_b, (k - 3) // 2 % 2, :, :, b, :],
                                rope_sum[rows_b].rearrange("p u t k -> p t u k"),
                                qb_tab[rows_b].rearrange("p u t k -> p t u k"), ALU.add).then_inc(q_bd_ready, 1)
                if runs(ii, k, PROB):
                    t = tile(ii, k, PROB)
                    r = (k - PROB) % 2
                    v = back_ps.rearrange("p (j c) -> p j c", c=32)[:, :, 0:2 * (HD + 1)].rearrange(
                        "p j (h c) -> p j h c", c=HD + 1)
                    m = inv[:, r, :].rearrange("p (j h) -> p j h", h=2)
                    dve.wait_ge(back_done, t + 1)
                    nc.vector.reciprocal(m, v[:, :, :, HD]).then_inc(inv_done, 1)
                    dve.wait_ge(inv_done, t + 1)
                    nc.vector.tensor_tensor(o[:, r, :].rearrange("p (j h c) -> p j h c", h=2, c=HD), v[:, :, :, 0:HD],
                                            m.unsqueeze(3).to_broadcast([P, 8, 2, HD]), ALU.mult).then_inc(o_ready, 1)

            steps(dve, step)

            dve.wait_ge(base_s, T)
            nc.vector.tensor_scalar(pad_at[:, 0:E], base[:], part[:], None, ALU.add).then_inc(lst, 1)
            nc.vector.tensor_scalar(pad_at[:, E:E + 1], part[:], float(E * REGION), None, ALU.add).then_inc(lst, 1)
            nc.vector.tensor_tensor(fill[:], base[:], bases[:], ALU.subtract).then_inc(lst, 1)
            dve.wait_ge(lst, 3)
            nc.vector.tensor_copy(pad_i[:], pad_at[:]).then_inc(pad_ready, 1)
            nc.vector.tensor_tensor(over[:], fill[:].unsqueeze(2).to_broadcast([P, E, T]),
                                    marks[:].unsqueeze(1).to_broadcast([P, E, T]), ALU.is_gt).then_inc(lst, 1)
            dve.wait_ge(lst, 4)
            nc.vector.tensor_reduce(blocks_of[:], over[:], AX.X, ALU.add).then_inc(lst, 1)
            dve.wait_ge(lst, 5)
            nc.vector.tensor_copy(ends[:], blocks_of[:]).then_inc(lst, 1)
            dve.wait_ge(lst, 6)
            n = 6
            src, dst = ends, ends_b
            for hop in (1, 2, 4):
                nc.vector.tensor_copy(dst[:, 0:hop], src[:, 0:hop]).then_inc(lst, 1)
                nc.vector.tensor_tensor(dst[:, hop:E], src[:, hop:E], src[:, 0:E - hop], ALU.add).then_inc(lst, 1)
                n += 2
                dve.wait_ge(lst, n)
                src, dst = dst, src
            nc.vector.tensor_tensor(passed[:], blk_iota[:].unsqueeze(2).to_broadcast([P, BLOCKS, E]),
                                    src[:].unsqueeze(1).to_broadcast([P, BLOCKS, E]), ALU.is_ge).then_inc(lst, 1)
            dve.wait_ge(lst, n + 1)
            nc.vector.tensor_reduce(blk_e[:], passed[:], AX.X, ALU.add).then_inc(lst, 1)
            nc.vector.tensor_tensor(passed_n[:], passed[:], blocks_of[:].unsqueeze(1).to_broadcast([P, BLOCKS, E]),
                                    ALU.mult).then_inc(lst, 1)
            dve.wait_ge(lst, n + 3)
            nc.vector.tensor_reduce(blk_first[:], passed_n[:], AX.X, ALU.add).then_inc(lst, 1)
            nc.vector.tensor_scalar(blk_live[:], blk_e[:], float(E), float(P), ALU.is_lt, ALU.mult).then_inc(lst, 1)
            nc.vector.tensor_scalar(blk_em[:], blk_e[:], float(E - 1), None, ALU.min).then_inc(lst, 1)
            dve.wait_ge(lst, n + 6)
            nc.vector.tensor_tensor(blk_rel[:], blk_iota[:], blk_first[:], ALU.subtract).then_inc(lst, 1)
            dve.wait_ge(lst, n + 7)
            nc.vector.tensor_tensor(blk_row[:], blk_rel[:], blk_live[:], ALU.mult).then_inc(lst, 1)
            nc.vector.tensor_copy(blk_e_i[:], blk_em[:]).then_inc(lst, 1)
            dve.wait_ge(lst, n + 9)
            nc.vector.scalar_tensor_tensor(blk_row_i[:], blk_e[:], float(REGION), blk_row[:],
                                           ALU.mult, ALU.add).then_inc(list_ready, 1)
            dve.wait_ge(list_ready, 1)
            dve.wait_ge(w_in2, 64)

            def block_step(ii, k):
                if block_runs(ii, k, HIDDEN):
                    j = block(ii, k, HIDDEN)
                    r = (k - HIDDEN) % 2
                    e = dve.value_load(blk_e_i[0:1, bass.ds(j, 1)], min_val=0, max_val=E - 1)
                    dve.wait_ge(h_done, j + 1)
                    nc.vector.tensor_tensor(hid[:, r, :], ps[:, r, :], b01[:, bass.ds(e * (2 * H), 2 * H)],
                                            ALU.add).then_inc(hb_done, 1)
                if block_runs(ii, k, RESULT):
                    j = block(ii, k, RESULT)
                    r = (k - RESULT) % 2
                    e = dve.value_load(blk_e_i[0:1, bass.ds(j, 1)], min_val=0, max_val=E - 1)
                    if block_runs(ii, k, RESULT + 4):
                        dve.wait_ge(y_out[(k - RESULT) % 4], 16 * (2 * ii + (k - RESULT) // 4))
                    nc.vector.tensor_copy(home_i[:, (k - RESULT) % 4, :], rows[:, (k - RESULT) % 8, D + 1:D + 2]).then_inc(home_done, 1)
                    dve.wait_ge(y_done, j + 1)
                    if block_runs(ii, k, RESULT + 2):
                        dve.wait_ge(yw_done, j - 1)
                    nc.vector.tensor_tensor(y[:, r, :], ps[:, 6 + r, 0:D], b2[:, bass.ds(e * D, D)],
                                            ALU.add).then_inc(yb_done, 1)
                if block_runs(ii, k, HIDDEN):
                    j = block(ii, k, HIDDEN)
                    r = (k - HIDDEN) % 2
                    dve.wait_ge(silu_done, j + 1)
                    if block_runs(ii, k, HIDDEN + 2):
                        dve.wait_ge(at_done, j - 1)
                    nc.vector.tensor_tensor(act_sb[:, r, :], hid[:, r, 0:H], silu[:, r, :], ALU.mult).then_inc(act_done, 1)

            block_steps(dve, block_step)

            def add_both(lap, k):
                dve.wait_ge(res_in[k], 32 * lap + 32)
                nc.vector.tensor_tensor(res[:, k, 0], res[:, k, 0], res[:, k, 1], ALU.add).then_inc(both, 1)

            for k in range(2):
                add_both(0, k)
            with dve.Fori(1, NC // 2) as lap:
                for k in range(2):
                    add_both(lap, k)


def kernel(**inputs):
    import numpy as _np
    import concourse.bacc as _bacc
    from concourse.bass_utils import run_bass_kernel_spmd as _run

    g = {n: _np.asarray(v) for n, v in inputs.items()}
    half_swap = (_np.arange(D) // HD) * HD + (_np.arange(D) % HD + HD // 2) % HD
    spread = _np.arange(D).reshape(NH // 2, 2, HD).transpose(1, 0, 2).ravel()

    def plain_and_swapped(w):
        return _np.stack([w.T, w[half_swap].T], axis=1)

    def bias_columns(b):
        return _np.stack([b, b[half_swap]]).reshape(2, 2, 64).transpose(2, 0, 1)

    inv_freq = (1.0 / _np.float32(10000.0) ** (_np.arange(0, HD, 2, dtype=_np.float32) / _np.float32(HD))).astype(_np.float32)
    angle = _np.arange(S, dtype=_np.float32)[None, :] * inv_freq[_np.arange(P) % (HD // 2)][:, None]
    sign = _np.where(_np.arange(P) % HD < HD // 2, -1.0, 1.0).astype(_np.float32)[:, None]
    turn = _np.stack([_np.cos(angle), _np.sin(angle) * sign], axis=1).astype(_np.float32)

    w0, w1, w2 = g["L0_ffn_w0"], g["L0_ffn_w1"], g["L0_ffn_w2"]
    arrays = {
        "x": g["x"], "ctx_1024": g["ctx_1024"], "g_xattn": g["g_xattn"], "g_ffn": g["g_ffn"],
        "wq": plain_and_swapped(g["L0_xattn_Wq"]), "wk": plain_and_swapped(g["L0_xattn_Wk"]),
        "qb": bias_columns(g["L0_xattn_bq"]), "kb": bias_columns(g["L0_xattn_bk"]),
        "wv": g["L0_xattn_Wv"].T[:, spread], "wo": g["L0_xattn_Wo"].T, "turn": turn,
        "L0_xattn_bv": g["L0_xattn_bv"], "L0_xattn_bo": g["L0_xattn_bo"],
        "gate_w": g["L0_ffn_gate_w"].T, "L0_ffn_gate_b": g["L0_ffn_gate_b"],
        "w01": _np.stack([w0, w1]).transpose(3, 1, 0, 2).reshape(D, -1),
        "b01": _np.stack([g["L0_ffn_b0"], g["L0_ffn_b1"]], axis=1).reshape(-1),
        "w2": w2.reshape(E, D, 2, H // 2).transpose(3, 0, 2, 1).reshape(H // 2, -1),
        "b2": g["L0_ffn_b2"].reshape(-1),
    }
    nc = _bacc.Bacc("TRN2", target_bir_lowering=False, num_devices=1)
    feeds, handles = {}, {}
    for name, v in arrays.items():
        v = _np.ascontiguousarray(v)
        feeds[f"in_{name}"] = v
        handles[name] = nc.dram_tensor(f"in_{name}", v.shape, mybir.dt.from_np(v.dtype), kind="ExternalInput").ap()
    out = nc.dram_tensor("out_0", (B, S, D), F32, kind="ExternalOutput").ap()
    flamingo_block(nc, handles, out)
    return _run(nc, [feeds], core_ids=[0]).results[0]["out_0"]
```

```python
from contextlib import ExitStack

import numpy as np

import concourse.bass as bass
from concourse import mybir

F32 = mybir.dt.float32
BF16 = mybir.dt.bfloat16
I32 = mybir.dt.int32
U32 = mybir.dt.uint32
ALU = mybir.AluOpType
ACT = mybir.ActivationFunctionType
AX = mybir.AxisListType.X

P = 128
D = 128
B, S = 128, 64
NH, HD = 16, 8
E, H = 8, 256
T = B * S // P
TOKENS = T * P
EPS = 1e-5
SCALE = HD ** -0.5

REGION = TOKENS + P
ROW = D + 2
BLOCKS = (2 * TOKENS + E * (P - 1)) // P + 1
BLOCKS += -BLOCKS % 8
NOWHERE = 2 * TOKENS

NORM1, XN, TURN, VALUE, SCORE, PROB, BACK, WO, GATE, TOP, SCATTER = 0, 1, 1, 2, 5, 6, 7, 8, 9, 10, 14
ROUTE = 13
LAP = 8
FILL = 2 * LAP
ROWS_T, META, HIDDEN, GLU, ACT_T, RESULT, OUT = 0, 1, 1, 2, 3, 4, 5
BLOCK_DRAIN = 5


def tile(ii, k, lag):
    return LAP * ii + (k - lag)


def rounds(ii, k, lag, ring):
    return LAP // ring * ii + (k - lag) // ring


def runs(ii, k, lag):
    return not isinstance(ii, int) or 0 <= LAP * ii + k - lag < T


def routes(ii, k):
    return (k - ROUTE) % 4 == 0 and runs(ii, k, ROUTE)


def steps(engine, step):
    for k in range(FILL + 1):
        step(0, k)
    with engine.Fori(FILL // LAP, T // LAP - 1) as ii:
        for k in range(1, LAP + 1):
            step(ii, k)
    for k in range(1, LAP + SCATTER):
        step(T // LAP - 1, k)


def block_steps(engine, lap):
    lap(0, 8)
    lap(1, 8)
    with engine.Fori(2, BLOCKS // 8) as ii:
        lap(ii, 8)
    lap(BLOCKS // 8, BLOCK_DRAIN)


def block(ii, k, lag):
    return 8 * ii + (k - lag)


def block_runs(ii, k, lag):
    return not isinstance(ii, int) or 0 <= 8 * ii + k - lag < BLOCKS


def flamingo_block(nc, a, out):
    with ExitStack() as ctx:
        def sb(name, shape, dt=F32):
            return ctx.enter_context(nc.sbuf_tensor(name, shape, dt))

        def sem(name):
            return ctx.enter_context(nc.semaphore(name))

        rows_dram = nc.dram_tensor("rows_by_expert", [E * REGION + P, ROW], F32, kind="Internal").ap()
        result_dram = nc.dram_tensor("results_by_slot", [2 * TOKENS, D], F32, kind="Internal").ap()

        ident = sb("ident", [P, P])
        before = sb("before", [P, 2, P], BF16)
        head_mask = sb("head_mask", [P, 8])
        mask_by_b = sb("mask_by_b", [P, 2, 8])
        iota8 = sb("iota8", [P, 4, 2, E])
        half = sb("half", [P, 1])
        wq = sb("wq", [P, 2, D])
        wk = sb("wk", [P, 2, D])
        wv = sb("wv", [P, D])
        wo = sb("wo", [P, D])
        wo_gated = sb("wo_gated", [P, D])
        turn_tab = sb("turn_tab", [P, 2, S])
        qb_col = sb("qb_col", [P, 2, 2])
        kb_col = sb("kb_col", [P, 2, 2])
        qb_tab = sb("qb_tab", [P, 2, 2, S])
        kb_tab = sb("kb_tab", [P, 2, 2, S])
        bt_tmp = sb("bt_tmp", [P, 2, S])
        bv_col = sb("bv_col", [P, 1])
        bv_wide = sb("bv_wide", [P, P])
        bo_wide = sb("bo_wide", [P, D])
        gates = sb("gates", [P, 2])
        tgate = sb("tgate", [P, 2])
        gate_w = sb("gate_w_sb", [P, E])
        gate_b = sb("gate_b_sb", [P, E])
        w01 = sb("w01", [P, E * 2 * H])
        b01 = sb("b01", [P, E * 2 * H])
        w2 = sb("w2_sb", [P, E * 2 * D])
        b2 = sb("b2_sb", [P, E * D])

        x = sb("x_sb", [P, T, D])
        ctx_in = sb("ctx_in", [P, 4, D])
        stats1 = sb("stats1", [P, 4, 6])
        mv1 = sb("mv1", [P, 4, 2])
        rstd1 = sb("rstd1", [P, 4, 2])
        xn = sb("xn", [P, 2, D])
        turned = sb("turned", [P, 4, 4, P])
        rope_mul = sb("rope_mul", [P, 2, 2, 2, S])
        rope_sum = sb("rope_sum", [P, 2, 2, S])
        q_part = sb("q_part", [P, 2, 2, S])
        k_rot = sb("k_rot", [P, 2, 2, S])[:]
        k_bd = sb("k_bd", [P, 2, 2, 2, 8, S])
        q_bd = sb("q_bd", [P, 2, 2, 2, 2, S])
        peak = sb("peak", [P, 2, NH])
        probs = sb("probs", [P, 2, 2, 8, S])
        probs_t = sb("probs_t", [P, 2, 8, P])
        v_bd = sb("v_bd", [P, 4, 2, 8, 32])
        mixed = sb("mixed", [P, 2, 2, P])
        inv = sb("inv", [P, 2, NH])
        o = sb("o_sb", [P, 2, D])
        stats2 = sb("stats2", [P, 4, 6])
        mv2 = sb("mv2", [P, 4, 2])
        rstd2 = sb("rstd2", [P, 4, 2])
        routed = sb("routed", [P, 8, 2, ROW])
        logits = sb("logits", [P, 2, E])
        top = sb("top", [P, 8, 8])
        top_at = sb("top_at", [P, 8, 8], U32)
        top_f = sb("top_f", [P, 4, 2])
        chosen = sb("chosen", [P, 4, 2, E])
        chosen_sum = sb("chosen_sum", [P, 4, E], BF16)
        gap = sb("gap", [P, 4])
        odds = sb("odds", [P, 4])
        odds1 = sb("odds1", [P, 4])
        share = sb("share", [P, 4])
        base = sb("base", [P, E])
        place = sb("place", [P, 4, E])
        place2 = sb("place2", [P, 4, 2, E])
        place_f = sb("place_f", [P, 4, 2])
        place_i = sb("place_i", [P, 8, 2], I32)
        home = sb("home", [P, T, 2])

        bases = sb("bases", [P, E])
        pad_i = sb("pad_i", [P, E], I32)
        pad_rows = sb("pad_rows", [P, ROW])
        fill = sb("fill", [P, E])
        marks = sb("marks", [P, T])
        over = sb("over", [P, E, T])
        blocks_of = sb("blocks_of", [P, E])
        ends = sb("ends", [P, E])
        ends_b = sb("ends_b", [P, E])
        blk_iota = sb("blk_iota", [P, BLOCKS])
        passed = sb("passed", [P, BLOCKS, E])
        passed_n = sb("passed_n", [P, BLOCKS, E])
        blk_e = sb("blk_e", [P, BLOCKS])
        blk_first = sb("blk_first", [P, BLOCKS])
        blk_live = sb("blk_live", [P, BLOCKS])
        blk_rel = sb("blk_rel", [P, BLOCKS])
        blk_row = sb("blk_row", [P, BLOCKS])
        blk_em = sb("blk_em", [P, BLOCKS])
        blk_e_i = sb("blk_e_i", [P, BLOCKS], I32)
        blk_row_i = sb("blk_row_i", [P, BLOCKS], I32)

        rows = sb("rows", [P, 8, ROW])
        rows_t = sb("rows_t", [P, 2, P])
        hid = sb("hid", [P, 2, 2 * H])
        silu = sb("silu", [P, 2, H])
        act_sb = sb("act_sb", [P, 2, H])
        act_t = sb("act_t", [P, 2, 2, P])
        y = sb("y_sb", [P, 2, D])
        yw = sb("yw", [P, 8, D])
        home_i = sb("home_i", [P, 8, 1], I32)
        weight = sb("weight", [P, 8, 1])

        CH = 4
        NC = T // CH
        res = sb("res", [P, 2, CH, 2, D])
        fin = sb("fin", [P, 2, CH, D])

        ps = ctx.enter_context(nc.psum_tensor("ps", [P, 8, 512], F32))
        score_ps = ps[:, 0:2, :]
        pt_ps = ps[:, 2:4, :]
        mix_ps = ps[:, 4, 0:256].rearrange("p (g q) -> p g q", g=2)
        val_ps = ps[:, 4, 256:384].rearrange("p (b j d) -> p b j d", b=2, d=HD)
        proj_ps = ps[:, 5, :]
        turn_ps = ps[:, 6, :]
        wo_ps = ps[:, 7, 0:128]
        gate_ps = ps[:, 7, 128:136]
        rank_ps = ps[:, 7, 136:168]
        total_ps = ps[:, 7, 168:176]
        back_ps = ps[:, 7, 256:512]

        w_in = sem("weights_in")
        w_in2 = sem("expert_weights_in")
        consts = sem("constants_made")
        p_set = sem("pool_setup_step")
        d_set = sem("dve_setup_step")
        setup = sem("setup_step")
        tanh_done = sem("tanh_done")
        bias_ps_done = sem("bias_product_done")
        setup_done = sem("setup_done")
        x_in = [sem(f"x_in{i}") for i in range(4)]
        c_in = [sem(f"ctx_in{i}") for i in range(4)]
        bn1 = sem("norm1_stats")
        agg1 = sem("norm1_aggregated")
        eps1 = sem("norm1_eps_added")
        pow1 = sem("norm1_rstd")
        xn_ready = sem("xn_ready")
        xb_ready = sem("x_plus_bias")
        turn_done = sem("turn_done")
        turned_ready = sem("turned_ready")
        proj_done = sem("proj_done")
        rope_muld = sem("rope_multiplied")
        rope_added = sem("rope_added")
        k_rot_ready = sem("k_rot_ready")
        k_bd_ready = sem("k_bd_ready")
        q_part_ready = sem("q_part_ready")
        q_bd_ready = sem("q_bd_ready")
        score_done = sem("score_done")
        peak_done = sem("peak_done")
        shifted = sem("scores_shifted")
        exp_done = sem("exp_done")
        pt_done = sem("probs_transposed")
        pt_ready = sem("probs_t_ready")
        mix_done = sem("values_and_mix_done")
        v_ready = sem("v_bd_ready")
        mixed_ready = sem("mixed_ready")
        back_done = sem("mix_turned_back")
        inv_done = sem("inverse_sum")
        o_ready = sem("o_ready")
        misc_done = sem("wo_gate_rank_done")
        x2_done = sem("x2_done")
        bn2 = sem("norm2_stats")
        agg2 = sem("norm2_aggregated")
        eps2 = sem("norm2_eps_added")
        pow2 = sem("norm2_rstd")
        xn2_ready = sem("xn2_ready")
        lg = sem("logits_ready")
        topd = sem("top_found")
        topi = sem("top_index_found")
        topf = sem("top_index_float")
        chose = sem("chosen_ready")
        chose_b = sem("chosen_sum_ready")
        gap_s = sem("gap_ready")
        odds_s = sem("odds_ready")
        odds1_s = sem("odds1_ready")
        share_s = sem("share_ready")
        w0_s = sem("first_weight_ready")
        w1_s = sem("second_weight_ready")
        place_s = sem("place_ready")
        base_s = sem("base_moved")
        place2_s = sem("place_masked")
        place_f_s = sem("place_summed")
        place_i_s = sem("place_index_ready")
        home_s = sem("home_written")
        scat = [sem(f"scattered{i}") for i in range(8)]
        pads = sem("pads_scattered")
        lst = sem("block_list_step")
        list_ready = sem("block_list_ready")
        pad_ready = sem("pad_ready")
        r_in = [sem(f"rows_in{i}") for i in range(8)]
        rt_done = sem("rows_turned")
        rt_ready = sem("rows_t_ready")
        h_done = sem("hidden_done")
        hb_done = sem("hidden_biased")
        silu_done = sem("silu_done")
        act_done = sem("act_done")
        at_done = sem("act_turned")
        at_ready = sem("act_t_ready")
        y_done = sem("y_done")
        yb_done = sem("y_biased")
        yw_done = sem("y_weighted")
        home_done = sem("home_index_ready")
        weight_done = sem("weight_copied")
        y_out = [sem(f"y_scattered{i}") for i in range(8)]
        res_in = [sem(f"results_in{i}") for i in range(2)]
        both = sem("both_experts_added")
        fin_done = sem("final_sum")
        stored = [sem(f"stored{i}") for i in range(2)]

        W_LOADS = 15
        program = ctx.enter_context(nc.Block())

        def wide(src, n):
            return src.rearrange("(a n) -> a n", a=1).to_broadcast([n, src.shape[0]])

        xd = a["x"].rearrange("b s d -> (b s) d")
        cd = a["ctx_1024"].rearrange("b s d -> (b s) d")
        od = out.rearrange("b s d -> (b s) d").rearrange("(t p) d -> p t d", p=P)

        def counted(engine, value):
            value = value if isinstance(value, int) else engine.to_reg(value)
            engine.wait_ge(setup_done, 1)
            return value

        def listed(engine, table, first, count, most):
            return list(nc.values_load_multi_w_load_instructions(
                table[0:1, bass.ds(first, count)], engines=(engine,), min_val=0, max_val=most)[1])

        def experts_of(engine, ii, count, behind):
            if isinstance(ii, int) and ii == 0:
                return [None] * behind + listed(engine, blk_e_i, 0, count, E - 1)
            return listed(engine, blk_e_i, 8 * ii - behind, behind + count - count % 8, E - 1)

        @program.sync
        def _(sp):
            sp.dma_start(wk[:], a["wk"]).then_inc(w_in, 16)
            sp.dma_start(wq[:], a["wq"]).then_inc(w_in, 16)
            sp.dma_start(wv[:], a["wv"]).then_inc(w_in, 16)
            sp.dma_start(wo[:], a["wo"]).then_inc(w_in, 16)
            sp.dma_start(turn_tab[:], a["turn"]).then_inc(w_in, 16)
            for b in range(2):
                sp.dma_start(qb_col[64 * b:64 * b + 64], a["qb"]).then_inc(w_in, 16)
                sp.dma_start(kb_col[64 * b:64 * b + 64], a["kb"]).then_inc(w_in, 16)
            sp.dma_start(bv_col[:], a["L0_xattn_bv"].rearrange("(d a) -> d a", a=1)).then_inc(w_in, 16)
            sp.dma_start(bo_wide[:], wide(a["L0_xattn_bo"], P)).then_inc(w_in, 16)
            sp.dma_start(gates[:, 0:1], wide(a["g_xattn"], P)).then_inc(w_in, 16)
            sp.dma_start(gates[:, 1:2], wide(a["g_ffn"], P)).then_inc(w_in, 16)
            sp.dma_start(gate_w[:], a["gate_w"]).then_inc(w_in, 16)
            sp.dma_start(gate_b[:], wide(a["L0_ffn_gate_b"], P)).then_inc(w_in, 16)

            def load(ii, k):
                t = tile(ii, k, NORM1)
                if runs(ii, k, NORM1 + 4):
                    sp.wait_ge(bn1, t - 3)
                    sp.wait_ge(turn_done, t - 3)
                sp.dma_start(x[:, t, :], xd[bass.ts(t, P), :]).then_inc(x_in[k % 4], 16)
                sp.dma_start(ctx_in[:, k % 4, :], cd[bass.ts(t, P), :]).then_inc(c_in[k % 4], 16)

            for k in range(4):
                load(0, k)
            sp.dma_start(w01[:], a["w01"]).then_inc(w_in2, 16)
            sp.dma_start(w2[:], a["w2"]).then_inc(w_in2, 16)
            sp.dma_start(b01[:], wide(a["b01"], P)).then_inc(w_in2, 16)
            sp.dma_start(b2[:], wide(a["b2"], P)).then_inc(w_in2, 16)
            for k in range(4, LAP):
                load(0, k)
            with sp.Fori(1, T // LAP) as ii:
                for k in range(LAP):
                    load(ii, k)

            sp.wait_ge(setup_done, 1)
            sp.dma_start(rows_dram[E * REGION:E * REGION + P, :], pad_rows[:]).then_inc(pads, 16)
            sp.wait_ge(pad_ready, 1)
            for quad in (0, 4):
                for at in listed(mybir.EngineType.SP, pad_i, quad, 4, (E - 1) * REGION + TOKENS):
                    sp.dma_start(rows_dram[bass.ds(at, P), :], pad_rows[:]).then_inc(pads, 16)

            sp.wait_ge(list_ready, 1)
            for q in scat:
                sp.wait_ge(q, 32 * T // 8)
            sp.wait_ge(pads, 16 * (E + 1))

            def load_blocks(lap, again):
                for quad in (0, 4):
                    at = listed(mybir.EngineType.SP, blk_row_i, 8 * lap + quad, 4, E * REGION)
                    for k in range(quad, quad + 4):
                        if again:
                            sp.wait_ge(weight_done, 8 * lap + k - 7)
                        sp.dma_start(rows[:, k, :], rows_dram[bass.ds(at[k - quad], P), :]).then_inc(r_in[k], 16)

            load_blocks(0, False)
            with sp.Fori(1, BLOCKS // 8) as lap:
                load_blocks(lap, True)

            for q in y_out:
                sp.wait_ge(q, 16 * BLOCKS // 8)
            rd = result_dram.rearrange("(p t s) d -> p t s d", s=2, p=P)

            def chunk(lap, k, again):
                c = 2 * lap + k
                if again:
                    sp.wait_ge(fin_done, c - 1)
                sp.dma_start(res[:, k], rd[:, bass.ds(CH * c, CH)]).then_inc(res_in[k], 16)

            def store(lap, k):
                c = 2 * lap + k
                sp.wait_ge(fin_done, c + 1)
                sp.dma_start(od[:, bass.ds(CH * c, CH), :], fin[:, k]).then_inc(stored[k], 16)

            for k in range(2):
                chunk(0, k, False)
            with sp.Fori(1, NC // 2) as lap:
                for k in range(2):
                    chunk(lap, k, True)
                    store(lap - 1, k)
            for k in range(2):
                store(NC // 2 - 1, k)
            for k in range(2):
                sp.wait_ge(stored[k], 16 * (NC // 2))

        @program.tensor
        def _(pe):
            pe.wait_ge(setup, 1)
            nc.tensor.matmul(wo_ps, bv_wide[:], wo[:], start=True, stop=True).then_inc(bias_ps_done, 1)
            pe.wait_ge(consts, 2)
            pe.wait_ge(setup_done, 1)

            def step(ii, k):
                s = LAP * ii + k
                if runs(ii, k, SCORE):
                    t = tile(ii, k, SCORE)
                    n = (k - SCORE) % 4 // 2
                    h = (k - SCORE) % 2
                    unit = LAP // 2 * ii + (k - SCORE) // 2
                    pe.wait_ge(q_bd_ready, 2 * unit + 2)
                    pe.wait_ge(k_bd_ready, 2 * unit + 2)
                    for u in range(2):
                        if runs(ii, k, SCORE + 1):
                            pe.wait_ge(shifted, 2 * t + u - 1)
                        nc.tensor.matmul(score_ps[:, u, :],
                                         q_bd[:, n, h, u].rearrange("p b q -> p (b q)"),
                                         k_bd[:, n, h, u].rearrange("p h k -> p (h k)"),
                                         start=True, stop=True).then_inc(score_done, 1)
                if runs(ii, k, PROB):
                    t = tile(ii, k, PROB)
                    r = (k - PROB) % 2
                    for u in range(2):
                        pe.wait_ge(exp_done, 2 * t + u + 1)
                        if runs(ii, k, PROB + 1):
                            pe.wait_ge(pt_ready, 2 * t + u - 1)
                        for j in range(4):
                            last = nc.tensor.transpose(
                                pt_ps[:, u, j * P:(j + 1) * P],
                                probs[:, r, u, 2 * j:2 * j + 2, :].rearrange("p h k -> p (h k)"), ident[:])
                        last.then_inc(pt_done, 1)
                if not isinstance(ii, int) or 1 <= s < T + GATE:
                    if not isinstance(ii, int) or s > 1:
                        pe.wait_ge(turned_ready, s - 1)
                    if runs(ii, k, TURN):
                        t = tile(ii, k, TURN)
                        r = (k - TURN) % 4
                        pe.wait_ge(xn_ready, t + 1)
                        last = nc.tensor.transpose(turn_ps[:, 0:128], xn[:, r % 2, :], ident[:])
                        pe.wait_ge(c_in[r], 16 * (rounds(ii, k, TURN, 4) + 1))
                        last = nc.tensor.transpose(turn_ps[:, 128:256], ctx_in[:, r, :], ident[:])
                    if runs(ii, k, WO):
                        pe.wait_ge(o_ready, tile(ii, k, WO) + 1)
                        last = nc.tensor.transpose(turn_ps[:, 256:384], o[:, (k - WO) % 2, :], ident[:])
                    if runs(ii, k, GATE):
                        pe.wait_ge(xn2_ready, tile(ii, k, GATE) + 1)
                        last = nc.tensor.transpose(turn_ps[:, 384:512], routed[:, (k - GATE) % 8, 0, 0:D], ident[:])
                    last.then_inc(turn_done, 1)
                if runs(ii, k, VALUE) or runs(ii, k, PROB):
                    if runs(ii, k, VALUE + 1):
                        pe.wait_ge(v_ready, tile(ii, k, VALUE))
                    if runs(ii, k, PROB + 1):
                        pe.wait_ge(mixed_ready, tile(ii, k, PROB))
                    if runs(ii, k, VALUE):
                        pe.wait_ge(turned_ready, s - 1)
                        for b in range(2):
                            for h in range(2):
                                last = nc.tensor.matmul(
                                    val_ps[64 * h:64 * h + 64, b].rearrange("p j d -> p (j d)"),
                                    turned[:, (k - VALUE) % 4, 1, 64 * b:64 * b + 64],
                                    wv[:, 64 * h:64 * h + 64], start=True, stop=True)
                    if runs(ii, k, PROB):
                        t = tile(ii, k, PROB)
                        pe.wait_ge(v_ready, t + 1)
                        for g in range(2):
                            pe.wait_ge(pt_ready, 2 * t + g + 1)
                            for b in range(2):
                                for j in range(4):
                                    last = nc.tensor.matmul(
                                        mix_ps[32 * j:32 * j + 32, g, 64 * b:64 * b + 64],
                                        v_bd[:, (k - PROB) % 4, b, 4 * g + j, :],
                                        probs_t[:, (k - PROB) % 2, 4 * g + j, 64 * b:64 * b + 64],
                                        start=True, stop=True)
                    last.then_inc(mix_done, 1)
                even = k % 2 == 0
                lag = 2 if even else 3
                if runs(ii, k, lag):
                    w, src = (wk, 1) if even else (wq, 0)
                    r = (k - lag) % 4
                    if not isinstance(ii, int) or s > 2:
                        pe.wait_ge(rope_muld, s - 2)
                    pe.wait_ge(turned_ready, s)
                    for turn in range(2):
                        for u in range(2):
                            for b in range(2):
                                last = nc.tensor.matmul(
                                    proj_ps[64 * b:64 * b + 64, 256 * turn + 128 * u:256 * turn + 128 * u + 128],
                                    w[:, turn, 64 * u:64 * u + 64],
                                    turned[:, r:r + 2, src, 64 * b:64 * b + 64],
                                    start=True, stop=True)
                    last.then_inc(proj_done, 1)
                if runs(ii, k, BACK) or runs(ii, k, WO) or runs(ii, k, GATE) or routes(ii, k):
                    if runs(ii, k, WO) or runs(ii, k, GATE):
                        pe.wait_ge(turned_ready, s)
                    if runs(ii, k, BACK + 1):
                        pe.wait_ge(o_ready, tile(ii, k, BACK))
                    elif runs(ii, k, WO + 1):
                        pe.wait_ge(x2_done, tile(ii, k, WO))
                    elif runs(ii, k, GATE + 1):
                        pe.wait_ge(lg, tile(ii, k, GATE))
                    if runs(ii, k, WO):
                        last = nc.tensor.matmul(wo_ps, turned[:, (k - TURN) % 4, 2, :], wo_gated[:],
                                                start=True, stop=True)
                    if runs(ii, k, GATE):
                        last = nc.tensor.matmul(gate_ps, turned[:, (k - TURN) % 4, 3, :], gate_w[:],
                                                start=True, stop=True)
                    if runs(ii, k, BACK):
                        pe.wait_ge(mixed_ready, tile(ii, k, BACK) + 1)
                        for g in range(2):
                            last = nc.tensor.transpose(back_ps[:, g * P:(g + 1) * P],
                                                       mixed[:, (k - BACK) % 2, g, :], ident[:])
                    if routes(ii, k):
                        pe.wait_ge(chose_b, rounds(ii, k, ROUTE, 4) + 1)
                        picks = chosen_sum[:].rearrange("p t e -> p (t e)")
                        nc.tensor.matmul(rank_ps, before[:, 0, :], picks, start=True, stop=False)
                        for j in range(1, 4):
                            nc.tensor.matmul(rank_ps[:, E * j:4 * E], before[:, 1, :], picks[:, 0:(4 - j) * E],
                                             start=False, stop=(j == 3))
                        for j in range(4):
                            last = nc.tensor.matmul(total_ps, before[:, 1, :], picks[:, E * j:E * j + E],
                                                    start=(j == 0), stop=(j == 3))
                    last.then_inc(misc_done, 1)

            steps(pe, step)

            pe.wait_ge(w_in2, 64)
            pe.wait_ge(list_ready, 1)

            def block_step(ii, k, experts):
                if block_runs(ii, k, HIDDEN):
                    j = block(ii, k, HIDDEN)
                    r = (k - HIDDEN) % 2
                    e = experts[k - HIDDEN + 4]
                    pe.wait_ge(rt_ready, j + 1)
                    if block_runs(ii, k, HIDDEN + 2):
                        pe.wait_ge(hb_done, j - 1)
                    nc.tensor.matmul(ps[:, r, :], rows_t[:, r, :], w01[:, bass.ds(e * (2 * H), 2 * H)],
                                     start=True, stop=True).then_inc(h_done, 1)
                if block_runs(ii, k, ROWS_T):
                    j = block(ii, k, ROWS_T)
                    pe.wait_ge(r_in[k], 16 * ii + 16)
                    if block_runs(ii, k, ROWS_T + 2):
                        pe.wait_ge(rt_ready, j - 1)
                    nc.tensor.transpose(ps[:, 2 + k % 2, 0:P], rows[:, k, 0:D], ident[:]).then_inc(rt_done, 1)
                if block_runs(ii, k, ACT_T):
                    j = block(ii, k, ACT_T)
                    r = (k - ACT_T) % 2
                    pe.wait_ge(act_done, j + 1)
                    if block_runs(ii, k, ACT_T + 2):
                        pe.wait_ge(at_ready, j - 1)
                    for c in range(2):
                        last = nc.tensor.transpose(ps[:, 4 + r, c * P:(c + 1) * P],
                                                   act_sb[:, r, c * P:(c + 1) * P], ident[:])
                    last.then_inc(at_done, 1)
                if block_runs(ii, k, RESULT):
                    j = block(ii, k, RESULT)
                    r = (k - RESULT) % 2
                    e = experts[k - RESULT + 4]
                    pe.wait_ge(at_ready, j + 1)
                    if block_runs(ii, k, RESULT + 2):
                        pe.wait_ge(yb_done, j - 1)
                    for c in range(2):
                        last = nc.tensor.matmul(ps[:, 6 + r, 0:D], act_t[:, r, c, :],
                                                w2[:, bass.ds(e * (2 * D) + c * D, D)], start=(c == 0), stop=(c == 1))
                    last.then_inc(y_done, 1)

            def lap(ii, count):
                experts = experts_of(mybir.EngineType.PE, ii, count, 4)
                for k in range(count):
                    block_step(ii, k, experts)

            block_steps(pe, lap)

        @program.scalar
        def _(act):
            act.wait_ge(w_in, 16 * W_LOADS)
            nc.scalar.activation(tgate[:], gates[:], ACT.Tanh).then_inc(tanh_done, 1)
            act.wait_ge(consts, 2)
            act.wait_ge(setup_done, 1)

            def spread_keys(ii, k, lag, heads):
                n = LAP // 2 * ii + (k - lag) // 2
                act.wait_ge(k_rot_ready, n + 1)
                if runs(ii, k, lag + 4):
                    act.wait_ge(score_done, 4 * n - 4)
                for h in heads:
                    last = nc.scalar.activation(k_bd[:, (k - lag) // 2 % 2, :, :, h, :],
                                                k_rot.rearrange("p u t k -> p t u k"), ACT.Copy,
                                                scale=head_mask[:, h:h + 1])
                last.then_inc(k_bd_ready, 1)

            def step(ii, k):
                s = LAP * ii + k
                if k % 2 == 0 and runs(ii, k, 4):
                    spread_keys(ii, k, 4, range(4, 8))
                if runs(ii, k, PROB):
                    t = tile(ii, k, PROB)
                    for u in range(2):
                        act.wait_ge(pt_done, 2 * t + u + 1)
                        nc.scalar.copy(probs_t[:, (k - PROB) % 2, 4 * u:4 * u + 4, :].rearrange("p j q -> p (j q)"),
                                       pt_ps[:, u, :]).then_inc(pt_ready, 1)
                if not isinstance(ii, int) or 1 <= s < T + GATE:
                    act.wait_ge(turn_done, s)
                    nc.scalar.copy(turned[:, (k - TURN) % 4].rearrange("p w t -> p (w t)"),
                                   turn_ps).then_inc(turned_ready, 1)
                if runs(ii, k, SCORE):
                    t = tile(ii, k, SCORE)
                    for u in range(2):
                        v = probs[:, (k - SCORE) % 2, u].rearrange("p h k -> p (h k)")
                        act.wait_ge(shifted, 2 * t + u + 1)
                        nc.scalar.activation(v, v, ACT.Exp, scale=SCALE).then_inc(exp_done, 1)
                if routes(ii, k):
                    act.wait_ge(gap_s, rounds(ii, k, ROUTE, 4) + 1)
                    nc.scalar.activation(odds[:], gap[:], ACT.Exp).then_inc(odds_s, 1)
                if runs(ii, k, VALUE) or runs(ii, k, PROB):
                    act.wait_ge(mix_done, s - VALUE + 1)
                    if runs(ii, k, VALUE):
                        for h in range(2):
                            last = nc.scalar.copy(
                                v_bd[64 * h:64 * h + 64, (k - VALUE) % 4, :, :, 9 * h:9 * h + HD],
                                val_ps[64 * h:64 * h + 64])
                        last.then_inc(v_ready, 1)
                    if runs(ii, k, PROB):
                        nc.scalar.copy(mixed[:, (k - PROB) % 2], mix_ps).then_inc(mixed_ready, 1)
                if k % 2 and runs(ii, k, 3):
                    spread_keys(ii, k, 3, range(4))

            steps(act, step)

            def block_step(ii, k):
                if block_runs(ii, k, OUT):
                    j = block(ii, k, OUT)
                    act.wait_ge(yb_done, j + 1)
                    nc.scalar.activation(yw[:, (k - OUT) % 8, :], y[:, (k - OUT) % 2, :], ACT.Copy,
                                         scale=weight[:, (k - OUT) % 8, :]).then_inc(yw_done, 1)
                if block_runs(ii, k, ROWS_T):
                    j = block(ii, k, ROWS_T)
                    act.wait_ge(rt_done, j + 1)
                    nc.scalar.copy(rows_t[:, k % 2, :], ps[:, 2 + k % 2, 0:P]).then_inc(rt_ready, 1)
                if block_runs(ii, k, ACT_T):
                    j = block(ii, k, ACT_T)
                    r = (k - ACT_T) % 2
                    act.wait_ge(at_done, j + 1)
                    nc.scalar.copy(act_t[:, r].rearrange("p c t -> p (c t)"),
                                   ps[:, 4 + r, 0:2 * P]).then_inc(at_ready, 1)
                if block_runs(ii, k, HIDDEN):
                    j = block(ii, k, HIDDEN)
                    r = (k - HIDDEN) % 2
                    act.wait_ge(hb_done, j + 1)
                    if block_runs(ii, k, HIDDEN + 2):
                        act.wait_ge(act_done, j - 1)
                    nc.scalar.activation(silu[:, r, :], hid[:, r, H:2 * H], ACT.Silu).then_inc(silu_done, 1)

            def lap(ii, count):
                for k in range(count):
                    block_step(ii, k)

            block_steps(act, lap)

        @program.gpsimd
        def _(pool):
            nc.gpsimd.memset(ident[:], 0.0).then_inc(p_set, 1)
            nc.gpsimd.memset(before[:], 1.0).then_inc(p_set, 1)
            nc.gpsimd.memset(mask_by_b[:], 1.0).then_inc(p_set, 1)
            nc.gpsimd.memset(half[:], -0.5).then_inc(p_set, 1)
            pool.wait_ge(p_set, 4)
            nc.gpsimd.affine_select(out=ident[:], in_=ident[:], compare_op=ALU.not_equal, fill=1.0, base=0,
                                    pattern=[[-1, P]], channel_multiplier=1).then_inc(consts, 1)
            nc.gpsimd.affine_select(out=before[:, 0, :], in_=before[:, 0, :], compare_op=ALU.is_gt, fill=0.0, base=0,
                                    pattern=[[1, P]], channel_multiplier=-1).then_inc(consts, 1)
            nc.gpsimd.affine_select(out=mask_by_b[:], in_=mask_by_b[:], compare_op=ALU.is_ge, fill=0.0, base=0,
                                    pattern=[[-64, 2], [-HD, 8]], channel_multiplier=1).then_inc(p_set, 1)
            pool.wait_ge(p_set, 5)
            nc.gpsimd.affine_select(out=mask_by_b[:], in_=mask_by_b[:], compare_op=ALU.is_ge, fill=0.0, base=HD - 1,
                                    pattern=[[64, 2], [HD, 8]], channel_multiplier=-1).then_inc(p_set, 1)
            nc.gpsimd.iota(iota8[:], [[0, 8], [1, E]], base=0, channel_multiplier=0,
                           allow_small_or_imprecise_dtypes=True).then_inc(p_set, 1)
            nc.gpsimd.iota(home[:], [[2, T], [1, 2]], base=0, channel_multiplier=2 * T,
                           allow_small_or_imprecise_dtypes=True).then_inc(p_set, 1)
            nc.gpsimd.iota(bases[:], [[REGION, E]], base=0, channel_multiplier=0,
                           allow_small_or_imprecise_dtypes=True).then_inc(p_set, 1)
            nc.gpsimd.iota(marks[:], [[P, T]], base=0, channel_multiplier=0,
                           allow_small_or_imprecise_dtypes=True).then_inc(p_set, 1)
            nc.gpsimd.iota(blk_iota[:], [[1, BLOCKS]], base=0, channel_multiplier=0,
                           allow_small_or_imprecise_dtypes=True).then_inc(p_set, 1)
            nc.gpsimd.memset(k_bd[:], 0.0).then_inc(p_set, 1)
            pool.wait_ge(setup_done, 1)

            def scatter(ii, k):
                due = counted(pool, rounds(ii, k, SCATTER, 4) + 1)
                r = (k - SCATTER) % 8
                pool.wait_ge(place_i_s, due)
                pool.wait_ge(home_s, due)
                pool.wait_ge(w1_s, due)
                for slot in range(2):
                    nc.gpsimd.indirect_dma_start(
                        out=rows_dram, out_offset=bass.IndirectOffsetOnAxis(ap=place_i[:, r, slot:slot + 1], axis=0),
                        in_=routed[:, r, slot, :], in_offset=None).then_inc(scat[r], 16)

            def power(mv, rstd, k, t, agg, eps, done):
                due = counted(pool, t + 1)
                pool.wait_ge(agg, due)
                nc.gpsimd.tensor_scalar(rstd[:, k, 0:1], mv[:, k, 1:2], EPS, None, ALU.add).then_inc(eps, 1)
                pool.wait_ge(eps, t + 1)
                nc.gpsimd.tensor_tensor(rstd[:, k, 1:2], rstd[:, k, 0:1], half[:], ALU.pow).then_inc(done, 1)

            def step(ii, k):
                if runs(ii, k, GATE):
                    power(mv2, rstd2, (k - GATE) % 4, tile(ii, k, GATE), agg2, eps2, pow2)
                if k % 2 and runs(ii, k, 3):
                    n = LAP // 2 * ii + (k - 3) // 2
                    pool.wait_ge(rope_added, n + 1)
                    if runs(ii, k, 5):
                        pool.wait_ge(k_bd_ready, 2 * n)
                    nc.gpsimd.tensor_tensor(k_rot, rope_sum[:], kb_tab[:], ALU.add).then_inc(k_rot_ready, 1)
                if k % 2 == 0 and runs(ii, k, 4):
                    n = LAP // 2 * ii + (k - 4) // 2
                    pool.wait_ge(rope_muld, 2 * n + 2)
                    if runs(ii, k, 6):
                        pool.wait_ge(q_bd_ready, 2 * n)
                    nc.gpsimd.tensor_tensor(q_part[:], rope_mul[:, 0], qb_tab[:], ALU.add).then_inc(q_part_ready, 1)
                if runs(ii, k, SCATTER):
                    scatter(ii, k)
                if runs(ii, k, NORM1):
                    power(mv1, rstd1, k % 4, tile(ii, k, NORM1), agg1, eps1, pow1)
                if runs(ii, k, 2):
                    t = tile(ii, k, 2)
                    pool.wait_ge(xn_ready, t + 1)
                    nc.gpsimd.tensor_tensor(x[:, t, :], x[:, t, :], bo_wide[:], ALU.add).then_inc(xb_ready, 1)

            steps(pool, step)

            def block_step(ii, k):
                if block_runs(ii, k, OUT):
                    j = block(ii, k, OUT)
                    r = (k - OUT) % 8
                    due = counted(pool, j + 1)
                    pool.wait_ge(yw_done, due)
                    pool.wait_ge(home_done, due)
                    nc.gpsimd.indirect_dma_start(
                        out=result_dram, out_offset=bass.IndirectOffsetOnAxis(ap=home_i[:, r, :], axis=0),
                        in_=yw[:, r, :], in_offset=None, bounds_check=2 * TOKENS - 1,
                        oob_is_err=False).then_inc(y_out[r], 16)

            def lap(ii, count):
                for k in range(count):
                    block_step(ii, k)

            block_steps(pool, lap)

            def finish(lap, k, again):
                c = 2 * lap + k
                pool.wait_ge(both, c + 1)
                if again:
                    pool.wait_ge(stored[k], 16 * lap)
                nc.gpsimd.tensor_tensor(fin[:, k], res[:, k, :, 0], x[:, bass.ds(CH * c, CH), :], ALU.add).then_inc(fin_done, 1)

            for k in range(2):
                finish(0, k, False)
            with pool.Fori(1, NC // 2) as lap:
                for k in range(2):
                    finish(lap, k, True)

        @program.vector
        def _(dve):
            nc.vector.memset(q_bd[:], 0.0).then_inc(d_set, 1)
            nc.vector.memset(v_bd[:], 0.0).then_inc(d_set, 1)
            nc.vector.memset(turn_ps, 0.0).then_inc(d_set, 1)
            nc.vector.memset(pad_rows[:], 0.0).then_inc(d_set, 1)
            nc.vector.memset(bv_wide[:], 1.0).then_inc(d_set, 1)
            dve.wait_ge(d_set, 5)
            nc.vector.memset(v_bd[0:64, :, :, :, HD:HD + 1], 1.0).then_inc(d_set, 1)
            nc.vector.memset(v_bd[64:128, :, :, :, 2 * HD + 1:2 * HD + 2], 1.0).then_inc(d_set, 1)
            nc.vector.memset(pad_rows[:, D + 1:D + 2], float(NOWHERE)).then_inc(d_set, 1)
            dve.wait_ge(w_in, 16 * W_LOADS)
            nc.vector.tensor_scalar(bv_wide[:], bv_wide[:], bv_col[:], None, ALU.mult).then_inc(setup, 1)
            dve.wait_ge(tanh_done, 1)
            nc.vector.tensor_scalar(wo_gated[:], wo[:], tgate[:, 0:1], None, ALU.mult).then_inc(d_set, 1)
            dve.wait_ge(bias_ps_done, 1)
            nc.vector.tensor_tensor(bo_wide[:], wo_ps, bo_wide[:], ALU.add).then_inc(d_set, 1)
            dve.wait_ge(d_set, 10)
            nc.vector.tensor_scalar(bo_wide[:], bo_wide[:], tgate[:, 0:1], None, ALU.mult).then_inc(d_set, 1)
            done = 11
            for col, tab in ((qb_col, qb_tab), (kb_col, kb_tab)):
                for u in range(2):
                    nc.vector.tensor_scalar(bt_tmp[:, u, :], turn_tab[:, 0, :], col[:, 0, u:u + 1],
                                            None, ALU.mult).then_inc(d_set, 1)
                    nc.vector.tensor_scalar(tab[:, u, 0, :], turn_tab[:, 1, :], col[:, 1, u:u + 1],
                                            None, ALU.mult).then_inc(d_set, 1)
                done += 4
                dve.wait_ge(d_set, done)
                nc.vector.tensor_tensor(tab[:, :, 1, :], tab[:, :, 0, :], bt_tmp[:], ALU.add).then_inc(d_set, 1)
                dve.wait_ge(d_set, done + 1)
                nc.vector.tensor_copy(tab[:, :, 0, :], tab[:, :, 1, :]).then_inc(d_set, 1)
                done += 2
                dve.wait_ge(d_set, done)
            dve.wait_ge(p_set, 12)
            nc.vector.tensor_tensor(head_mask[:], mask_by_b[:, 0], mask_by_b[:, 1], ALU.add).then_inc(d_set, 1)
            dve.wait_ge(d_set, done + 1)
            nc.vector.tensor_copy(base[:], bases[:]).then_inc(setup_done, 1)
            dve.wait_ge(setup_done, 1)

            def step(ii, k):
                s = LAP * ii + k
                lag = 3 if k % 2 else 4
                if runs(ii, k, lag):
                    n = LAP // 2 * ii + (k - lag) // 2
                    dve.wait_ge(proj_done, s - 2)
                    nc.vector.tensor_tensor(
                        rope_mul[:].rearrange("p w u t k -> p w (u t) k"),
                        proj_ps.rearrange("p (w c k) -> p w c k", w=2, k=S),
                        turn_tab[:].unsqueeze(2).to_broadcast([P, 2, 4, S]), ALU.mult).then_inc(rope_muld, 1)
                if runs(ii, k, XN):
                    t = tile(ii, k, XN)
                    dve.wait_ge(pow1, t + 1)
                    if runs(ii, k, XN + 2):
                        dve.wait_ge(turn_done, s - 2)
                    nc.vector.tensor_scalar(xn[:, (k - XN) % 2, :], x[:, t, :], mv1[:, (k - XN) % 4, 0:1],
                                            rstd1[:, (k - XN) % 4, 1:2], ALU.subtract, ALU.mult).then_inc(xn_ready, 1)
                if k % 2 and runs(ii, k, lag):
                    dve.wait_ge(rope_muld, s - 2)
                    if runs(ii, k, lag + 2):
                        dve.wait_ge(k_rot_ready, n)
                    nc.vector.tensor_tensor(rope_sum[:], rope_mul[:, 0], rope_mul[:, 1], ALU.add).then_inc(rope_added, 1)
                if runs(ii, k, GATE):
                    t = tile(ii, k, GATE)
                    r = (k - GATE) % 4
                    q = (k - GATE) % 8
                    dve.wait_ge(pow2, t + 1)
                    if runs(ii, k, GATE + 8):
                        dve.wait_ge(scat[q], 32 * rounds(ii, k, GATE, 8))
                    nc.vector.tensor_scalar(routed[:, q, :, 0:D], x[:, t, :].unsqueeze(1).to_broadcast([P, 2, D]),
                                            mv2[:, r, 0:1], rstd2[:, r, 1:2], ALU.subtract, ALU.mult).then_inc(xn2_ready, 1)
                if runs(ii, k, SCORE):
                    t = tile(ii, k, SCORE)
                    r = (k - SCORE) % 2
                    for u in range(2):
                        v = score_ps[:, u, :].rearrange("p (h k) -> p h k", h=8)
                        m = peak[:, r, 8 * u:8 * u + 8]
                        dve.wait_ge(score_done, 2 * t + u + 1)
                        nc.vector.tensor_reduce(m, v, AX.X, ALU.max).then_inc(peak_done, 1)
                        dve.wait_ge(peak_done, 2 * t + u + 1)
                        nc.vector.tensor_tensor(probs[:, r, u], v, m.unsqueeze(2).to_broadcast([P, 8, S]),
                                                ALU.subtract).then_inc(shifted, 1)
                if k % 2 == 0 and runs(ii, k, lag):
                    dve.wait_ge(q_part_ready, n + 1)
                    if runs(ii, k, lag + 4):
                        dve.wait_ge(score_done, 4 * n - 4)
                    for b in range(2):
                        rows_b = slice(64 * b, 64 * b + 64)
                        nc.vector.tensor_tensor(
                            q_bd[rows_b, (k - lag) // 2 % 2, :, :, b, :],
                            q_part[rows_b].rearrange("p u t k -> p t u k"),
                            rope_mul[rows_b, 1].rearrange("p u t k -> p t u k"), ALU.add).then_inc(q_bd_ready, 1)
                if runs(ii, k, NORM1):
                    t = tile(ii, k, NORM1)
                    due = counted(dve, 16 * (rounds(ii, k, NORM1, 4) + 1))
                    dve.wait_ge(x_in[k % 4], due)
                    nc.vector.bn_stats(stats1[:, k % 4, :], x[:, t, :]).then_inc(bn1, 1)
                if runs(ii, k, TOP):
                    due = counted(dve, tile(ii, k, TOP) + 1)
                    dve.wait_ge(lg, due)
                    nc.vector.max(top[:, (k - TOP) % 8, :], logits[:, (k - TOP) % 2, :]).then_inc(topd, 1)
                if runs(ii, k, NORM1):
                    due = counted(dve, tile(ii, k, NORM1) + 1)
                    dve.wait_ge(bn1, due)
                    nc.vector.bn_aggr(mv1[:, k % 4, :], stats1[:, k % 4, :]).then_inc(agg1, 1)
                if runs(ii, k, TOP):
                    due = counted(dve, tile(ii, k, TOP) + 1)
                    dve.wait_ge(topd, due)
                    nc.vector.max_index(top_at[:, (k - TOP) % 8, :], top[:, (k - TOP) % 8, :],
                                        logits[:, (k - TOP) % 2, :]).then_inc(topi, 1)
                if routes(ii, k):
                    g = rounds(ii, k, ROUTE, 4)
                    q = (k - ROUTE) % 8
                    nc.vector.tensor_tensor(gap[:], top[:, q:q + 4, 1], top[:, q:q + 4, 0], ALU.subtract).then_inc(gap_s, 1)
                    dve.wait_ge(topi, 4 * g + 4)
                    nc.vector.tensor_copy(top_f[:], top_at[:, q:q + 4, 0:2]).then_inc(topf, 1)
                    dve.wait_ge(topf, g + 1)
                    nc.vector.tensor_tensor(chosen[:], iota8[:], top_f[:].unsqueeze(3).to_broadcast([P, 4, 2, E]),
                                            ALU.is_equal).then_inc(chose, 1)
                    dve.wait_ge(chose, g + 1)
                    nc.vector.tensor_tensor(chosen_sum[:], chosen[:, :, 0], chosen[:, :, 1], ALU.add).then_inc(chose_b, 1)
                if runs(ii, k, BACK) or runs(ii, k, WO) or runs(ii, k, GATE) or routes(ii, k):
                    dve.wait_ge(misc_done, s - BACK + 1)
                if routes(ii, k):
                    nc.vector.tensor_tensor(place[:], rank_ps.rearrange("p (t e) -> p t e", e=E),
                                            base[:].unsqueeze(1).to_broadcast([P, 4, E]), ALU.add).then_inc(place_s, 1)
                if runs(ii, k, WO):
                    t = tile(ii, k, WO)
                    dve.wait_ge(xb_ready, t + 1)
                    nc.vector.tensor_tensor(x[:, t, :], wo_ps, x[:, t, :], ALU.add).then_inc(x2_done, 1)
                if runs(ii, k, GATE):
                    nc.vector.tensor_tensor(logits[:, (k - GATE) % 2, :], gate_ps, gate_b[:], ALU.add).then_inc(lg, 1)
                if routes(ii, k):
                    dve.wait_ge(place_s, g + 1)
                    nc.vector.tensor_tensor(base[:], total_ps, base[:], ALU.add).then_inc(base_s, 1)
                if runs(ii, k, BACK):
                    r = (k - BACK) % 2
                    v = back_ps.rearrange("p (j c) -> p j c", c=32)[:, :, 0:2 * (HD + 1)].rearrange(
                        "p j (h c) -> p j h c", c=HD + 1)
                    m = inv[:, r, :].rearrange("p (j h) -> p j h", h=2)
                    nc.vector.reciprocal(m, v[:, :, :, HD]).then_inc(inv_done, 1)
                if runs(ii, k, WO):
                    t = tile(ii, k, WO)
                    due = counted(dve, t + 1)
                    dve.wait_ge(x2_done, due)
                    nc.vector.bn_stats(stats2[:, (k - WO) % 4, :], x[:, t, :]).then_inc(bn2, 1)
                if runs(ii, k, BACK):
                    dve.wait_ge(inv_done, tile(ii, k, BACK) + 1)
                    nc.vector.tensor_tensor(o[:, r, :].rearrange("p (j h c) -> p j h c", h=2, c=HD), v[:, :, :, 0:HD],
                                            m.unsqueeze(3).to_broadcast([P, 8, 2, HD]), ALU.mult).then_inc(o_ready, 1)
                if runs(ii, k, WO):
                    due = counted(dve, tile(ii, k, WO) + 1)
                    dve.wait_ge(bn2, due)
                    nc.vector.bn_aggr(mv2[:, (k - WO) % 4, :], stats2[:, (k - WO) % 4, :]).then_inc(agg2, 1)
                if routes(ii, k):
                    tiles = slice(q, q + 4)
                    nc.vector.tensor_tensor(place2[:], chosen[:], place[:].unsqueeze(2).to_broadcast([P, 4, 2, E]),
                                            ALU.mult).then_inc(place2_s, 1)
                    dve.wait_ge(odds_s, g + 1)
                    nc.vector.tensor_scalar(odds1[:], odds[:], 1.0, None, ALU.add).then_inc(odds1_s, 1)
                    dve.wait_ge(place2_s, g + 1)
                    nc.vector.tensor_reduce(place_f[:], place2[:], AX.X, ALU.add).then_inc(place_f_s, 1)
                    dve.wait_ge(odds1_s, g + 1)
                    nc.vector.reciprocal(share[:], odds1[:]).then_inc(share_s, 1)
                    dve.wait_ge(place_f_s, g + 1)
                    nc.vector.tensor_copy(place_i[:, tiles, :], place_f[:]).then_inc(place_i_s, 1)
                    dve.wait_ge(share_s, g + 1)
                    nc.vector.tensor_scalar(routed[:, tiles, 0, D], share[:], tgate[:, 1:2], None,
                                            ALU.mult).then_inc(w0_s, 1)
                    nc.vector.tensor_copy(routed[:, tiles, :, D + 1],
                                          home[:, bass.ds(4 * g, 4), :]).then_inc(home_s, 1)
                    dve.wait_ge(w0_s, g + 1)
                    nc.vector.tensor_tensor(routed[:, tiles, 1, D], routed[:, tiles, 0, D], odds[:],
                                            ALU.mult).then_inc(w1_s, 1)

            steps(dve, step)

            dve.wait_ge(base_s, T // 4)
            nc.vector.tensor_copy(pad_i[:], base[:]).then_inc(pad_ready, 1)
            nc.vector.tensor_tensor(fill[:], base[:], bases[:], ALU.subtract).then_inc(lst, 1)
            dve.wait_ge(lst, 1)
            nc.vector.tensor_tensor(over[:], fill[:].unsqueeze(2).to_broadcast([P, E, T]),
                                    marks[:].unsqueeze(1).to_broadcast([P, E, T]), ALU.is_gt).then_inc(lst, 1)
            dve.wait_ge(lst, 2)
            nc.vector.tensor_reduce(blocks_of[:], over[:], AX.X, ALU.add).then_inc(lst, 1)
            dve.wait_ge(lst, 3)
            nc.vector.tensor_copy(ends[:], blocks_of[:]).then_inc(lst, 1)
            dve.wait_ge(lst, 4)
            n = 4
            src, dst = ends, ends_b
            for hop in (1, 2, 4):
                nc.vector.tensor_copy(dst[:, 0:hop], src[:, 0:hop]).then_inc(lst, 1)
                nc.vector.tensor_tensor(dst[:, hop:E], src[:, hop:E], src[:, 0:E - hop], ALU.add).then_inc(lst, 1)
                n += 2
                dve.wait_ge(lst, n)
                src, dst = dst, src
            nc.vector.tensor_tensor(passed[:], blk_iota[:].unsqueeze(2).to_broadcast([P, BLOCKS, E]),
                                    src[:].unsqueeze(1).to_broadcast([P, BLOCKS, E]), ALU.is_ge).then_inc(lst, 1)
            dve.wait_ge(lst, n + 1)
            nc.vector.tensor_reduce(blk_e[:], passed[:], AX.X, ALU.add).then_inc(lst, 1)
            nc.vector.tensor_tensor(passed_n[:], passed[:], blocks_of[:].unsqueeze(1).to_broadcast([P, BLOCKS, E]),
                                    ALU.mult).then_inc(lst, 1)
            dve.wait_ge(lst, n + 3)
            nc.vector.tensor_reduce(blk_first[:], passed_n[:], AX.X, ALU.add).then_inc(lst, 1)
            nc.vector.tensor_scalar(blk_live[:], blk_e[:], float(E), float(P), ALU.is_lt, ALU.mult).then_inc(lst, 1)
            nc.vector.tensor_scalar(blk_em[:], blk_e[:], float(E - 1), None, ALU.min).then_inc(lst, 1)
            dve.wait_ge(lst, n + 6)
            nc.vector.tensor_tensor(blk_rel[:], blk_iota[:], blk_first[:], ALU.subtract).then_inc(lst, 1)
            dve.wait_ge(lst, n + 7)
            nc.vector.tensor_tensor(blk_row[:], blk_rel[:], blk_live[:], ALU.mult).then_inc(lst, 1)
            nc.vector.tensor_copy(blk_e_i[:], blk_em[:]).then_inc(lst, 1)
            dve.wait_ge(lst, n + 9)
            nc.vector.scalar_tensor_tensor(blk_row_i[:], blk_e[:], float(REGION), blk_row[:],
                                           ALU.mult, ALU.add).then_inc(list_ready, 1)
            dve.wait_ge(list_ready, 1)
            dve.wait_ge(w_in2, 64)

            def block_step(ii, k, experts):
                if block_runs(ii, k, OUT):
                    j = block(ii, k, OUT)
                    e = experts[k - OUT + 8]
                    dve.wait_ge(y_done, j + 1)
                    if block_runs(ii, k, OUT + 2):
                        dve.wait_ge(yw_done, j - 1)
                    nc.vector.tensor_tensor(y[:, (k - OUT) % 2, :], ps[:, 6 + (k - OUT) % 2, 0:D], b2[:, bass.ds(e * D, D)],
                                            ALU.add).then_inc(yb_done, 1)
                if block_runs(ii, k, META):
                    j = block(ii, k, META)
                    q = (k - META) % 8
                    dve.wait_ge(rt_done, j + 1)
                    if block_runs(ii, k, META + 8):
                        dve.wait_ge(y_out[q], 16 * (ii + (k - META) // 8))
                    nc.vector.tensor_copy(home_i[:, q, :], rows[:, q, D + 1:D + 2]).then_inc(home_done, 1)
                    nc.vector.tensor_copy(weight[:, q, :], rows[:, q, D:D + 1]).then_inc(weight_done, 1)
                if block_runs(ii, k, GLU):
                    j = block(ii, k, GLU)
                    r = (k - GLU) % 2
                    dve.wait_ge(silu_done, j + 1)
                    if block_runs(ii, k, GLU + 2):
                        dve.wait_ge(at_done, j - 1)
                    nc.vector.tensor_tensor(act_sb[:, r, :], hid[:, r, 0:H], silu[:, r, :], ALU.mult).then_inc(act_done, 1)
                if block_runs(ii, k, HIDDEN):
                    j = block(ii, k, HIDDEN)
                    r = (k - HIDDEN) % 2
                    e = experts[k - HIDDEN + 8]
                    dve.wait_ge(h_done, j + 1)
                    nc.vector.tensor_tensor(hid[:, r, :], ps[:, r, :], b01[:, bass.ds(e * (2 * H), 2 * H)],
                                            ALU.add).then_inc(hb_done, 1)

            def lap(ii, count):
                experts = experts_of(mybir.EngineType.DVE, ii, count, 8)
                for k in range(count):
                    block_step(ii, k, experts)

            block_steps(dve, lap)

            def add_both(lap, k):
                dve.wait_ge(res_in[k], 16 * lap + 16)
                nc.vector.tensor_tensor(res[:, k, :, 0], res[:, k, :, 0], res[:, k, :, 1], ALU.add).then_inc(both, 1)

            for k in range(2):
                add_both(0, k)
            with dve.Fori(1, NC // 2) as lap:
                for k in range(2):
                    add_both(lap, k)


def kernel(**inputs):
    import numpy as _np
    import concourse.bacc as _bacc
    from concourse.bass_utils import run_bass_kernel_spmd as _run

    g = {n: _np.asarray(v) for n, v in inputs.items()}
    half_swap = (_np.arange(D) // HD) * HD + (_np.arange(D) % HD + HD // 2) % HD
    spread = _np.arange(D).reshape(NH // 2, 2, HD).transpose(1, 0, 2).ravel()

    def plain_and_swapped(w):
        return _np.stack([w.T, w[half_swap].T], axis=1)

    def bias_columns(b):
        return _np.stack([b, b[half_swap]]).reshape(2, 2, 64).transpose(2, 0, 1)

    inv_freq = (1.0 / _np.float32(10000.0) ** (_np.arange(0, HD, 2, dtype=_np.float32) / _np.float32(HD))).astype(_np.float32)
    angle = _np.arange(S, dtype=_np.float32)[None, :] * inv_freq[_np.arange(P) % (HD // 2)][:, None]
    sign = _np.where(_np.arange(P) % HD < HD // 2, -1.0, 1.0).astype(_np.float32)[:, None]
    turn = _np.stack([_np.cos(angle), _np.sin(angle) * sign], axis=1).astype(_np.float32)

    w0, w1, w2 = g["L0_ffn_w0"], g["L0_ffn_w1"], g["L0_ffn_w2"]
    arrays = {
        "x": g["x"], "ctx_1024": g["ctx_1024"], "g_xattn": g["g_xattn"], "g_ffn": g["g_ffn"],
        "wq": plain_and_swapped(g["L0_xattn_Wq"]), "wk": plain_and_swapped(g["L0_xattn_Wk"]),
        "qb": bias_columns(g["L0_xattn_bq"]), "kb": bias_columns(g["L0_xattn_bk"]),
        "wv": g["L0_xattn_Wv"].T[:, spread], "wo": g["L0_xattn_Wo"].T, "turn": turn,
        "L0_xattn_bv": g["L0_xattn_bv"], "L0_xattn_bo": g["L0_xattn_bo"],
        "gate_w": g["L0_ffn_gate_w"].T, "L0_ffn_gate_b": g["L0_ffn_gate_b"],
        "w01": _np.stack([w0, w1]).transpose(3, 1, 0, 2).reshape(D, -1),
        "b01": _np.stack([g["L0_ffn_b0"], g["L0_ffn_b1"]], axis=1).reshape(-1),
        "w2": w2.reshape(E, D, 2, H // 2).transpose(3, 0, 2, 1).reshape(H // 2, -1),
        "b2": g["L0_ffn_b2"].reshape(-1),
    }
    nc = _bacc.Bacc("TRN2", target_bir_lowering=False, num_devices=1)
    feeds, handles = {}, {}
    for name, v in arrays.items():
        v = _np.ascontiguousarray(v)
        feeds[f"in_{name}"] = v
        handles[name] = nc.dram_tensor(f"in_{name}", v.shape, mybir.dt.from_np(v.dtype), kind="ExternalInput").ap()
    out = nc.dram_tensor("out_0", (B, S, D), F32, kind="ExternalOutput").ap()
    flamingo_block(nc, handles, out)
    return _run(nc, [feeds], core_ids=[0]).results[0]["out_0"]
```

```python
from contextlib import ExitStack

import numpy as np

import concourse.bass as bass
from concourse import mybir

F32 = mybir.dt.float32
BF16 = mybir.dt.bfloat16
I32 = mybir.dt.int32
U32 = mybir.dt.uint32
ALU = mybir.AluOpType
ACT = mybir.ActivationFunctionType
AX = mybir.AxisListType.X

P = 128
D = 128
B, S = 128, 64
NH, HD = 16, 8
E, H = 8, 256
T = B * S // P
TOKENS = T * P
EPS = 1e-5
SCALE = HD ** -0.5

REGION = TOKENS + P
ROW = D + 2
BLOCKS = (2 * TOKENS + E * (P - 1)) // P + 1
BLOCKS += -BLOCKS % 8
NOWHERE = 2 * TOKENS

NORM1, XN, TURN, VALUE, SCORE, PROB, BACK, WO, XN2, GATE, TOP, SCATTER = -1, 0, 1, 3, 6, 7, 8, 9, 10, 11, 12, 17
ROUTE, PLACE = 15, 16
LAP = 8
FIRST = 2
FILL = 2 * LAP + FIRST
ROWS_T, META, HIDDEN, GLU, ACT_T, RESULT = 0, 1, 1, 2, 3, 4
BLOCK_DRAIN = 4


def tile(ii, k, lag):
    return LAP * ii + (k - lag)


def rounds(ii, k, lag, ring):
    return LAP // ring * ii + (k - lag) // ring


def runs(ii, k, lag):
    return not isinstance(ii, int) or 0 <= LAP * ii + k - lag < T


def groups(ii, k, lag):
    return (k - lag) % 4 == 0 and runs(ii, k, lag)


def steps(engine, step):
    for k in range(NORM1, FILL):
        step(0, k)
    with engine.Fori(FILL // LAP, T // LAP - 1) as ii:
        for k in range(FIRST, LAP + FIRST):
            step(ii, k)
    for k in range(FIRST, LAP + SCATTER):
        step(T // LAP - 1, k)


def block_steps(engine, lap):
    def pair(ii, count):
        words = lap(ii, 8, ahead=True)
        lap(ii + 1, count, words)

    pair(0, 8)
    with engine.Fori(1, BLOCKS // 16) as jj:
        pair(2 * jj, 8)
    pair(BLOCKS // 8 - 1, BLOCK_DRAIN)


def block(ii, k, lag):
    return 8 * ii + (k - lag)


def block_runs(ii, k, lag):
    return not isinstance(ii, int) or 0 <= 8 * ii + k - lag < BLOCKS


assert BLOCKS // 8 % 2 == 1


def flamingo_block(nc, a, out):
    with ExitStack() as ctx:
        def sb(name, shape, dt=F32):
            return ctx.enter_context(nc.sbuf_tensor(name, shape, dt))

        def sem(name):
            return ctx.enter_context(nc.semaphore(name))

        rows_dram = nc.dram_tensor("rows_by_expert", [E * REGION + P, ROW], F32, kind="Internal").ap()
        result_dram = nc.dram_tensor("results_by_slot", [2 * TOKENS, D], F32, kind="Internal").ap()

        by_row = sb("by_row", [P, 7 * D + E + 9])
        alike = sb("alike", [P, D + E + 2])
        wk = by_row[:, 0:2 * D].rearrange("p (w e) -> p w e", w=2)
        wq = by_row[:, 2 * D:4 * D].rearrange("p (w e) -> p w e", w=2)
        wv = by_row[:, 4 * D:5 * D]
        wo = by_row[:, 5 * D:6 * D]
        turn_tab = by_row[:, 6 * D:7 * D].rearrange("p (w s) -> p w s", w=2)
        gate_w = by_row[:, 7 * D:7 * D + E]
        kb_col = by_row[:, 7 * D + E:7 * D + E + 4].rearrange("p (w u) -> p w u", w=2)
        qb_col = by_row[:, 7 * D + E + 4:7 * D + E + 8].rearrange("p (w u) -> p w u", w=2)
        bv_col = by_row[:, 7 * D + E + 8:7 * D + E + 9]
        bo_wide = alike[:, 0:D]
        gate_b = alike[:, D:D + E]
        gates = alike[:, D + E:D + E + 2]
        ident = sb("ident", [P, P])
        before = sb("before", [P, 2, P], BF16)
        head_mask = sb("head_mask", [P, 8])
        mask_by_b = sb("mask_by_b", [P, 2, 8])
        iota8 = sb("iota8", [P, 4, 2, E])
        minus_half = sb("minus_half", [P, 2])
        minus_one = sb("minus_one", [P, 4])
        one = sb("one", [P, 4])
        eps = sb("eps", [P, 2])
        wo_gated = sb("wo_gated", [P, D])
        qb_tab = sb("qb_tab", [P, 2, 2, S])
        kb_tab = sb("kb_tab", [P, 2, 2, S])
        bt_tmp = sb("bt_tmp", [P, 2, S])
        bv_wide = sb("bv_wide", [P, P])
        tgate = sb("tgate", [P, 2])
        w01 = sb("w01", [P, E * 2 * H])
        b01 = sb("b01", [P, E * 2 * H])
        w2 = sb("w2_sb", [P, E * 2 * D])
        b2 = sb("b2_sb", [P, E * D])

        x = sb("x_sb", [P, T, D])
        ctx_in = sb("ctx_in", [P, 4, D])
        stats = sb("stats", [P, 4, 2, 6])
        mv = sb("mv", [P, 4, 2, 2])
        var_eps = sb("var_eps", [P, 4, 2])
        rstd = sb("rstd", [P, 4, 2])
        neg_mean = sb("neg_mean", [P, 4])
        shift1 = sb("shift1", [P, 4])
        xn = sb("xn", [P, 2, D])
        turned = sb("turned", [P, 4, 4, P])
        rope_mul = sb("rope_mul", [P, 2, 2, 2, S])
        rope_sum = sb("rope_sum", [P, 2, 2, S])
        q_part = sb("q_part", [P, 2, 2, S])
        k_rot = sb("k_rot", [P, 2, 2, S])[:]
        k_bd = sb("k_bd", [P, 2, 2, 2, 8, S])
        q_bd = sb("q_bd", [P, 2, 2, 2, 2, S])
        peak = sb("peak", [P, 2, 2, 8])
        probs = sb("probs", [P, 2, 2, 8, S])
        probs_t = sb("probs_t", [P, 2, 8, P])
        v_bd = sb("v_bd", [P, 4, 2, 8, 32])
        mixed = sb("mixed", [P, 2, 2, P])
        inv = sb("inv", [P, 2, NH])
        o = sb("o_sb", [P, 2, D])
        routed = sb("routed", [P, 8, 2, ROW])
        logits = sb("logits", [P, 2, E])
        top = sb("top", [P, 8, 8])
        top_at = sb("top_at", [P, 8, 8], U32)
        top_f = sb("top_f", [P, 4, 2])
        chosen = sb("chosen", [P, 4, 2, E])
        chosen_sum = sb("chosen_sum", [P, 4, E], BF16)
        gap = sb("gap", [P, 4])
        odds = sb("odds", [P, 4])
        odds1 = sb("odds1", [P, 4])
        share = sb("share", [P, 4])
        base = sb("base", [P, E])
        place = sb("place", [P, 4, E])
        place2 = sb("place2", [P, 4, 2, E])
        place_f = sb("place_f", [P, 4, 2])
        place_i = sb("place_i", [P, 8, 2], I32)
        home = sb("home", [P, T, 2])

        bases = sb("bases", [P, E])
        pad_i = sb("pad_i", [P, E], I32)
        pad_rows = sb("pad_rows", [P, ROW])
        fill = sb("fill", [P, E])
        marks = sb("marks", [P, T])
        over = sb("over", [P, E, T])
        blocks_of = sb("blocks_of", [P, E])
        ends = sb("ends", [P, E])
        ends_b = sb("ends_b", [P, E])
        blk_iota = sb("blk_iota", [P, BLOCKS])
        passed = sb("passed", [P, BLOCKS, E])
        passed_n = sb("passed_n", [P, BLOCKS, E])
        blk_e = sb("blk_e", [P, BLOCKS])
        blk_first = sb("blk_first", [P, BLOCKS])
        blk_live = sb("blk_live", [P, BLOCKS])
        blk_rel = sb("blk_rel", [P, BLOCKS])
        blk_row = sb("blk_row", [P, BLOCKS])
        blk_em = sb("blk_em", [P, BLOCKS])
        place_value = sb("place_value", [P, 8])
        digits = sb("digits", [P, BLOCKS])
        lap_experts = sb("lap_experts", [P, BLOCKS // 8])
        lap_experts_i = sb("lap_experts_i", [P, BLOCKS // 8 + 1], I32)
        blk_row_i = sb("blk_row_i", [P, BLOCKS], I32)

        rows = sb("rows", [P, 8, ROW])
        rows_t = sb("rows_t", [P, 2, P])
        hid = sb("hid", [P, 2, 2 * H])
        silu = sb("silu", [P, 2, H])
        act_sb = sb("act_sb", [P, 2, H])
        act_t = sb("act_t", [P, 2, 2, P])
        y = sb("y_sb", [P, 2, D])
        yw = sb("yw", [P, 8, D])
        home_i = sb("home_i", [P, 8, 1], I32)
        weight = sb("weight", [P, 8, 1])

        CH = 4
        CHUNKS = T // CH
        res = k_bd[:].rearrange("p n t u h k -> p (n t u h k)").rearrange("p (r t s d) -> p r t s d", r=4, t=CH, s=2)

        ps = ctx.enter_context(nc.psum_tensor("ps", [P, 8, 512], F32))
        score_ps = ps[:, 0:2, :]
        pt_ps = ps[:, 2:4, :]
        mix_ps = ps[:, 4, 0:256].rearrange("p (g q) -> p g q", g=2)
        val_ps = ps[:, 4, 256:384].rearrange("p (b j d) -> p b j d", b=2, d=HD)
        proj_ps = ps[:, 5, :]
        turn_ps = ps[:, 6, :]
        wo_ps = ps[:, 7, 0:128]
        gate_ps = ps[:, 7, 128:136]
        rank_ps = ps[:, 7, 136:168]
        total_ps = ps[:, 7, 168:176]
        back_ps = ps[:, 7, 256:512]

        w_in = sem("weights_in")
        w_in2 = sem("expert_weights_in")
        consts = sem("constants_made")
        p_set = sem("pool_setup_step")
        d_set = sem("dve_setup_step")
        setup = sem("setup_step")
        tanh_done = sem("tanh_done")
        bias_ps_done = sem("bias_product_done")
        setup_done = sem("setup_done")
        x_in = [sem(f"x_in{i}") for i in range(4)]
        c_in = [sem(f"ctx_in{i}") for i in range(4)]
        bn1 = sem("norm1_stats")
        agg1 = sem("norm1_aggregated")
        xn_ready = sem("xn_ready")
        xb_ready = sem("x_plus_bias")
        turn_done = sem("turn_done")
        turned_ready = sem("turned_ready")
        proj_done = sem("proj_done")
        rope_muld = sem("rope_multiplied")
        rope_added = sem("rope_added")
        k_rot_ready = sem("k_rot_ready")
        k_bd_ready = sem("k_bd_ready")
        q_part_ready = sem("q_part_ready")
        q_bd_ready = sem("q_bd_ready")
        score_done = sem("score_done")
        peak_done = sem("peak_done")
        shifted = sem("scores_shifted")
        exp_done = sem("exp_done")
        pt_done = sem("probs_transposed")
        pt_ready = sem("probs_t_ready")
        mix_done = sem("values_and_mix_done")
        v_ready = sem("v_bd_ready")
        mixed_ready = sem("mixed_ready")
        inv_done = sem("inverse_sum")
        o_ready = sem("o_ready")
        misc_done = sem("wo_gate_rank_done")
        x2_done = sem("x2_done")
        bn2 = sem("norm2_stats")
        agg2 = sem("norm2_aggregated")
        eps_done = sem("eps_added")
        neg_done = sem("mean_negated")
        rstd_done = sem("rstd_ready")
        shift_done = sem("first_norm_shift_ready")
        xn2_ready = sem("xn2_ready")
        lg = sem("logits_ready")
        topd = sem("top_found")
        topi = sem("top_index_found")
        topf = sem("top_index_float")
        chose = sem("chosen_ready")
        chose_b = sem("chosen_sum_ready")
        gap_s = sem("gap_ready")
        odds_s = sem("odds_ready")
        odds1_s = sem("odds1_ready")
        share_s = sem("share_ready")
        w0_s = sem("first_weight_ready")
        w1_s = sem("second_weight_ready")
        place_s = sem("place_ready")
        base_s = sem("base_moved")
        place2_s = sem("place_masked")
        place_f_s = sem("place_summed")
        place_i_s = sem("place_index_ready")
        home_s = sem("home_written")
        scat = [sem(f"scattered{i}") for i in range(8)]
        pads = sem("pads_scattered")
        lst = sem("block_list_step")
        list_ready = sem("block_list_ready")
        pad_ready = sem("pad_ready")
        r_in = [sem(f"rows_in{i}") for i in range(8)]
        rt_done = sem("rows_turned")
        rt_ready = sem("rows_t_ready")
        h_done = sem("hidden_done")
        hb_done = sem("hidden_biased")
        silu_done = sem("silu_done")
        act_done = sem("act_done")
        at_done = sem("act_turned")
        at_ready = sem("act_t_ready")
        y_done = sem("y_done")
        yb_done = sem("y_biased")
        yw_done = sem("y_weighted")
        home_done = sem("home_index_ready")
        weight_done = sem("weight_copied")
        y_out = [sem(f"y_scattered{i}") for i in range(8)]
        res_in = [sem(f"results_in{i}") for i in range(4)]
        both = sem("both_experts_added")
        fin_done = sem("final_sum")
        stored = [sem(f"stored{i}") for i in range(4)]

        W_LOADS = 2
        program = ctx.enter_context(nc.Block())

        def wide(src, n):
            return src.rearrange("(a n) -> a n", a=1).to_broadcast([n, src.shape[0]])

        xd = a["x"].rearrange("b s d -> (b s) d")
        cd = a["ctx_1024"].rearrange("b s d -> (b s) d")
        od = out.rearrange("b s d -> (b s) d").rearrange("(t p) d -> p t d", p=P)

        def counted(engine, value):
            value = value if isinstance(value, int) else engine.to_reg(value)
            engine.wait_ge(setup_done, 1)
            return value

        def listed(engine, table, first, count, most):
            return list(nc.values_load_multi_w_load_instructions(
                table[0:1, bass.ds(first, count)], engines=(engine,), min_val=0, max_val=most)[1])

        def lap_word(engine, ii):
            return listed(engine, lap_experts_i, ii + 1, 1, E ** 8 - 1)[0]

        def last_and_this_lap(engine, ii):
            if isinstance(ii, int) and ii == 0:
                return None, lap_word(engine, ii)
            return listed(engine, lap_experts_i, ii, 2, E ** 8 - 1)

        def experts_near(words):
            before_lap, now = words

            def expert(i):
                word = now if i >= 0 else before_lap
                return word // E ** (i % 8) % E
            return expert

        @program.sync
        def _(sp):
            sp.dma_start(by_row[:], a["by_row"]).then_inc(w_in, 16)
            sp.dma_start(alike[:], wide(a["alike"], P)).then_inc(w_in, 16)

            def load_expert(e, part):
                if part == 0:
                    sp.dma_start(w01[:, bass.ts(e, 2 * H)], a["w01"][:, bass.ts(e, 2 * H)]).then_inc(w_in2, 16)
                elif part == 1:
                    sp.dma_start(w2[:, bass.ts(e, 2 * D)], a["w2"][:, bass.ts(e, 2 * D)]).then_inc(w_in2, 16)
                elif part == 2:
                    sp.dma_start(b01[:, bass.ts(e, 2 * H)], wide(a["b01"][bass.ts(e, 2 * H)], P)).then_inc(w_in2, 16)
                elif part == 3:
                    sp.dma_start(b2[:, bass.ts(e, D)], wide(a["b2"][bass.ts(e, D)], P)).then_inc(w_in2, 16)

            def load(ii, k):
                t = tile(ii, k, 0)
                if runs(ii, k, 4):
                    sp.wait_ge(bn1, t - 3)
                    sp.wait_ge(turn_done, t - 3)
                sp.dma_start(x[:, t, :], xd[bass.ts(t, P), :]).then_inc(x_in[k % 4], 16)
                sp.dma_start(ctx_in[:, k % 4, :], cd[bass.ts(t, P), :]).then_inc(c_in[k % 4], 16)

            for k in range(LAP):
                load(0, k)
            for part in range(4):
                load_expert(0, part)
            with sp.Fori(1, E) as ii:
                for k in range(LAP):
                    load(ii, k)
                    load_expert(ii, k)

            sp.wait_ge(setup_done, 1)
            sp.dma_start(rows_dram[E * REGION:E * REGION + P, :], pad_rows[:]).then_inc(pads, 16)
            sp.wait_ge(pad_ready, 1)
            for quad in (0, 4):
                for at in listed(mybir.EngineType.SP, pad_i, quad, 4, (E - 1) * REGION + TOKENS):
                    sp.dma_start(rows_dram[bass.ds(at, P), :], pad_rows[:]).then_inc(pads, 16)

            sp.wait_ge(list_ready, 2)
            for q in scat:
                sp.wait_ge(q, 32 * T // 8)
            sp.wait_ge(pads, 16 * (E + 1))

            def load_blocks(lap, again):
                for quad in (0, 4):
                    at = listed(mybir.EngineType.SP, blk_row_i, 8 * lap + quad, 4, E * REGION)
                    for k in range(quad, quad + 4):
                        if again:
                            sp.wait_ge(weight_done, 8 * lap + k - 7)
                        sp.dma_start(rows[:, k, :], rows_dram[bass.ds(at[k - quad], P), :]).then_inc(r_in[k], 16)

            load_blocks(0, False)
            with sp.Fori(1, BLOCKS // 8) as lap:
                load_blocks(lap, True)

            for q in y_out:
                sp.wait_ge(q, 16 * BLOCKS // 8)
            rd = result_dram.rearrange("(p t s) d -> p t s d", s=2, p=P)

            def chunk(lap, k, again):
                c = 4 * lap + k
                if again:
                    sp.wait_ge(fin_done, c - 3)
                sp.dma_start(res[:, k], rd[:, bass.ds(CH * c, CH)]).then_inc(res_in[k], 16)

            def store(lap, k):
                c = 4 * lap + k
                sp.wait_ge(fin_done, c + 1)
                sp.dma_start(od[:, bass.ds(CH * c, CH), :], x[:, bass.ds(CH * c, CH), :]).then_inc(stored[k], 16)

            for k in range(4):
                chunk(0, k, False)
            with sp.Fori(1, CHUNKS // 4) as lap:
                for k in range(4):
                    store(lap - 1, k)
                    chunk(lap, k, True)
            for k in range(4):
                store(CHUNKS // 4 - 1, k)
            for k in range(4):
                sp.wait_ge(stored[k], 16 * (CHUNKS // 4))

        @program.tensor
        def _(pe):
            pe.wait_ge(setup, 1)
            nc.tensor.matmul(wo_ps, bv_wide[:], wo, start=True, stop=True).then_inc(bias_ps_done, 1)
            pe.wait_ge(consts, 2)
            pe.wait_ge(setup_done, 1)

            def step(ii, k):
                s = LAP * ii + k
                if runs(ii, k, SCORE):
                    t = tile(ii, k, SCORE)
                    n = (k - SCORE) % 4 // 2
                    h = (k - SCORE) % 2
                    unit = LAP // 2 * ii + (k - SCORE) // 2
                    pe.wait_ge(q_bd_ready, 2 * unit + 2)
                    pe.wait_ge(k_bd_ready, 2 * unit + 2)
                    if runs(ii, k, SCORE + 1):
                        pe.wait_ge(shifted, t)
                    for u in range(2):
                        nc.tensor.matmul(score_ps[:, u, :],
                                         q_bd[:, n, h, u].rearrange("p b q -> p (b q)"),
                                         k_bd[:, n, h, u].rearrange("p h k -> p (h k)"),
                                         start=True, stop=True).then_inc(score_done, 1)
                if runs(ii, k, PROB):
                    t = tile(ii, k, PROB)
                    r = (k - PROB) % 2
                    for u in range(2):
                        pe.wait_ge(exp_done, 2 * t + u + 1)
                        if runs(ii, k, PROB + 1):
                            pe.wait_ge(pt_ready, 2 * t + u - 1)
                        for j in range(4):
                            last = nc.tensor.transpose(
                                pt_ps[:, u, j * P:(j + 1) * P],
                                probs[:, r, u, 2 * j:2 * j + 2, :].rearrange("p h k -> p (h k)"), ident[:])
                        last.then_inc(pt_done, 1)
                if not isinstance(ii, int) or 1 <= s < T + GATE:
                    if not isinstance(ii, int) or s > 1:
                        pe.wait_ge(turned_ready, s - 1)
                    if runs(ii, k, TURN):
                        t = tile(ii, k, TURN)
                        r = (k - TURN) % 4
                        pe.wait_ge(xn_ready, t + 1)
                        last = nc.tensor.transpose(turn_ps[:, 0:128], xn[:, r % 2, :], ident[:])
                        pe.wait_ge(c_in[r], 16 * (rounds(ii, k, TURN, 4) + 1))
                        last = nc.tensor.transpose(turn_ps[:, 128:256], ctx_in[:, r, :], ident[:])
                    if runs(ii, k, WO):
                        pe.wait_ge(o_ready, tile(ii, k, WO) + 1)
                        last = nc.tensor.transpose(turn_ps[:, 256:384], o[:, (k - WO) % 2, :], ident[:])
                    if runs(ii, k, GATE):
                        pe.wait_ge(xn2_ready, tile(ii, k, GATE) + 1)
                        last = nc.tensor.transpose(turn_ps[:, 384:512], routed[:, (k - GATE) % 8, 0, 0:D], ident[:])
                    last.then_inc(turn_done, 1)
                if runs(ii, k, VALUE) or runs(ii, k, PROB):
                    if runs(ii, k, VALUE + 1):
                        pe.wait_ge(v_ready, tile(ii, k, VALUE))
                    if runs(ii, k, PROB + 1):
                        pe.wait_ge(mixed_ready, tile(ii, k, PROB))
                    if runs(ii, k, VALUE):
                        pe.wait_ge(turned_ready, s - 1)
                        for b in range(2):
                            for h in range(2):
                                last = nc.tensor.matmul(
                                    val_ps[64 * h:64 * h + 64, b].rearrange("p j d -> p (j d)"),
                                    turned[:, (k - VALUE) % 4, 1, 64 * b:64 * b + 64],
                                    wv[:, 64 * h:64 * h + 64], start=True, stop=True)
                    if runs(ii, k, PROB):
                        t = tile(ii, k, PROB)
                        pe.wait_ge(v_ready, t + 1)
                        for g in range(2):
                            pe.wait_ge(pt_ready, 2 * t + g + 1)
                            for b in range(2):
                                for j in range(4):
                                    last = nc.tensor.matmul(
                                        mix_ps[32 * j:32 * j + 32, g, 64 * b:64 * b + 64],
                                        v_bd[:, (k - PROB) % 4, b, 4 * g + j, :],
                                        probs_t[:, (k - PROB) % 2, 4 * g + j, 64 * b:64 * b + 64],
                                        start=True, stop=True)
                    last.then_inc(mix_done, 1)
                even = k % 2 == 0
                lag = 2 if even else 3
                if runs(ii, k, lag):
                    w, src = (wk, 1) if even else (wq, 0)
                    r = (k - lag) % 4
                    if not isinstance(ii, int) or s > 2:
                        pe.wait_ge(rope_muld, s - 2)
                    pe.wait_ge(turned_ready, s)
                    for turn in range(2):
                        for u in range(2):
                            for b in range(2):
                                last = nc.tensor.matmul(
                                    proj_ps[64 * b:64 * b + 64, 256 * turn + 128 * u:256 * turn + 128 * u + 128],
                                    w[:, turn, 64 * u:64 * u + 64],
                                    turned[:, r:r + 2, src, 64 * b:64 * b + 64],
                                    start=True, stop=True)
                    last.then_inc(proj_done, 1)
                if runs(ii, k, BACK) or runs(ii, k, WO) or runs(ii, k, GATE) or groups(ii, k, PLACE):
                    if runs(ii, k, WO) or runs(ii, k, GATE):
                        pe.wait_ge(turned_ready, s)
                    if runs(ii, k, BACK + 1):
                        pe.wait_ge(o_ready, tile(ii, k, BACK))
                    elif runs(ii, k, WO + 1):
                        pe.wait_ge(x2_done, tile(ii, k, WO))
                    elif runs(ii, k, GATE + 1):
                        pe.wait_ge(lg, tile(ii, k, GATE))
                    if isinstance(ii, int) and groups(ii, k - 1, PLACE):
                        pe.wait_ge(base_s, rounds(ii, k - 1, PLACE, 4) + 1)
                    if runs(ii, k, BACK):
                        pe.wait_ge(mixed_ready, tile(ii, k, BACK) + 1)
                        for g in range(2):
                            last = nc.tensor.transpose(back_ps[:, g * P:(g + 1) * P],
                                                       mixed[:, (k - BACK) % 2, g, :], ident[:])
                    if runs(ii, k, WO):
                        last = nc.tensor.matmul(wo_ps, turned[:, (k - TURN) % 4, 2, :], wo_gated[:],
                                                start=True, stop=True)
                    if runs(ii, k, GATE):
                        last = nc.tensor.matmul(gate_ps, turned[:, (k - TURN) % 4, 3, :], gate_w,
                                                start=True, stop=True)
                    if groups(ii, k, PLACE):
                        pe.wait_ge(chose_b, rounds(ii, k, PLACE, 4) + 1)
                        picks = chosen_sum[:].rearrange("p t e -> p (t e)")
                        nc.tensor.matmul(rank_ps, before[:, 0, :], picks, start=True, stop=False)
                        for j in range(1, 4):
                            nc.tensor.matmul(rank_ps[:, E * j:4 * E], before[:, 1, :], picks[:, 0:(4 - j) * E],
                                             start=False, stop=(j == 3))
                        for j in range(4):
                            last = nc.tensor.matmul(total_ps, before[:, 1, :], picks[:, E * j:E * j + E],
                                                    start=(j == 0), stop=(j == 3))
                    last.then_inc(misc_done, 1)

            steps(pe, step)

            pe.wait_ge(w_in2, 64 * E)
            pe.wait_ge(list_ready, 2)

            def block_step(ii, k, expert, hidden_at):
                if block_runs(ii, k, ROWS_T):
                    j = block(ii, k, ROWS_T)
                    pe.wait_ge(r_in[k], 16 * ii + 16)
                    if block_runs(ii, k, ROWS_T + 2):
                        pe.wait_ge(rt_ready, j - 1)
                    nc.tensor.transpose(ps[:, 2 + k % 2, 0:P], rows[:, k, 0:D], ident[:]).then_inc(rt_done, 1)
                if block_runs(ii, k, ACT_T):
                    j = block(ii, k, ACT_T)
                    r = (k - ACT_T) % 2
                    pe.wait_ge(act_done, j + 1)
                    if block_runs(ii, k, ACT_T + 2):
                        pe.wait_ge(at_ready, j - 1)
                    for c in range(2):
                        last = nc.tensor.transpose(ps[:, 4 + r, c * P:(c + 1) * P],
                                                   act_sb[:, r, c * P:(c + 1) * P], ident[:])
                    last.then_inc(at_done, 1)
                if block_runs(ii, k, HIDDEN):
                    j = block(ii, k, HIDDEN)
                    r = (k - HIDDEN) % 2
                    pe.wait_ge(rt_ready, j + 1)
                    if block_runs(ii, k, HIDDEN + 2):
                        pe.wait_ge(hb_done, j - 1)
                    nc.tensor.matmul(ps[:, r, :], rows_t[:, r, :], w01[:, bass.ds(hidden_at, 2 * H)],
                                     start=True, stop=True).then_inc(h_done, 1)
                result_at = next_at = None
                if block_runs(ii, k, RESULT):
                    result_at = nc.snap(expert(k - RESULT) * (2 * D), engines=[mybir.EngineType.PE])
                if k < 7 and block_runs(ii, k + 1, HIDDEN):
                    next_at = nc.snap(expert(k + 1 - HIDDEN) * (2 * H), engines=[mybir.EngineType.PE])
                if block_runs(ii, k, RESULT):
                    j = block(ii, k, RESULT)
                    r = (k - RESULT) % 2
                    pe.wait_ge(at_ready, j + 1)
                    if block_runs(ii, k, RESULT + 2):
                        pe.wait_ge(yb_done, j - 1)
                    for c in range(2):
                        last = nc.tensor.matmul(ps[:, 6 + r, 0:D], act_t[:, r, c, :],
                                                w2[:, bass.ds(result_at + c * D, D)], start=(c == 0), stop=(c == 1))
                    last.then_inc(y_done, 1)

                return next_at

            def lap(ii, count, words=None, ahead=False):
                words = words or last_and_this_lap(mybir.EngineType.PE, ii)
                expert, next_words = experts_near(words), (words[1], None)
                hidden_at = expert(-HIDDEN) * (2 * H) if block_runs(ii, 0, HIDDEN) else None
                for k in range(count):
                    hidden_at = block_step(ii, k, expert, hidden_at)
                    if ahead and k == 4 and block_runs(ii, 8, ROWS_T):
                        next_words = (words[1], lap_word(mybir.EngineType.PE, ii + 1))
                return next_words

            block_steps(pe, lap)

        @program.scalar
        def _(act):
            act.wait_ge(w_in, 16 * W_LOADS)
            nc.scalar.activation(tgate[:], gates, ACT.Tanh).then_inc(tanh_done, 1)
            act.wait_ge(consts, 2)
            act.wait_ge(setup_done, 1)

            def spread_keys(ii, k, lag, heads):
                n = LAP // 2 * ii + (k - lag) // 2
                act.wait_ge(k_rot_ready, n + 1)
                if runs(ii, k, lag + 4):
                    act.wait_ge(score_done, 4 * n - 4)
                for h in heads:
                    last = nc.scalar.activation(k_bd[:, (k - lag) // 2 % 2, :, :, h, :],
                                                k_rot.rearrange("p u t k -> p t u k"), ACT.Copy,
                                                scale=head_mask[:, h:h + 1])
                last.then_inc(k_bd_ready, 1)

            def step(ii, k):
                s = LAP * ii + k
                if runs(ii, k, PROB):
                    t = tile(ii, k, PROB)
                    for u in range(2):
                        act.wait_ge(pt_done, 2 * t + u + 1)
                        nc.scalar.copy(probs_t[:, (k - PROB) % 2, 4 * u:4 * u + 4, :].rearrange("p j q -> p (j q)"),
                                       pt_ps[:, u, :]).then_inc(pt_ready, 1)
                if not isinstance(ii, int) or 1 <= s < T + GATE:
                    act.wait_ge(turn_done, s)
                    nc.scalar.copy(turned[:, (k - TURN) % 4].rearrange("p w t -> p (w t)"),
                                   turn_ps).then_inc(turned_ready, 1)
                if runs(ii, k, VALUE) or runs(ii, k, PROB):
                    act.wait_ge(mix_done, s - VALUE + 1)
                    if runs(ii, k, VALUE):
                        for h in range(2):
                            last = nc.scalar.copy(
                                v_bd[64 * h:64 * h + 64, (k - VALUE) % 4, :, :, 9 * h:9 * h + HD],
                                val_ps[64 * h:64 * h + 64])
                        last.then_inc(v_ready, 1)
                    if runs(ii, k, PROB):
                        nc.scalar.copy(mixed[:, (k - PROB) % 2], mix_ps).then_inc(mixed_ready, 1)
                if runs(ii, k, XN):
                    r = (k - XN - 1) % 4
                    act.wait_ge(shift_done, s + 1)
                    if runs(ii, k, XN + 2):
                        act.wait_ge(turn_done, s - 1)
                    nc.scalar.activation(xn[:, k % 2, :], x[:, tile(ii, k, XN), :], ACT.Identity,
                                         bias=shift1[:, r:r + 1], scale=rstd[:, r, 0:1]).then_inc(xn_ready, 1)
                if runs(ii, k, SCORE):
                    t = tile(ii, k, SCORE)
                    act.wait_ge(shifted, t + 1)
                    for u in range(2):
                        v = probs[:, (k - SCORE) % 2, u].rearrange("p h k -> p (h k)")
                        nc.scalar.activation(v, v, ACT.Exp, scale=SCALE).then_inc(exp_done, 1)
                if runs(ii, k, 3 + (k + 1) % 2):
                    spread_keys(ii, k, 3 + (k + 1) % 2, range(4 * ((k + 1) % 2) + 0, 4 * ((k + 1) % 2) + 4))
                if groups(ii, k, ROUTE):
                    act.wait_ge(gap_s, rounds(ii, k, ROUTE, 4) + 1)
                    nc.scalar.activation(odds[:], gap[:], ACT.Exp).then_inc(odds_s, 1)

            steps(act, step)

            def block_step(ii, k):
                if block_runs(ii, k, ROWS_T):
                    j = block(ii, k, ROWS_T)
                    act.wait_ge(rt_done, j + 1)
                    nc.scalar.copy(rows_t[:, k % 2, :], ps[:, 2 + k % 2, 0:P]).then_inc(rt_ready, 1)
                if block_runs(ii, k, ACT_T):
                    j = block(ii, k, ACT_T)
                    r = (k - ACT_T) % 2
                    act.wait_ge(at_done, j + 1)
                    nc.scalar.copy(act_t[:, r].rearrange("p c t -> p (c t)"),
                                   ps[:, 4 + r, 0:2 * P]).then_inc(at_ready, 1)
                if block_runs(ii, k, HIDDEN):
                    j = block(ii, k, HIDDEN)
                    r = (k - HIDDEN) % 2
                    act.wait_ge(hb_done, j + 1)
                    if block_runs(ii, k, HIDDEN + 2):
                        act.wait_ge(act_done, j - 1)
                    nc.scalar.activation(silu[:, r, :], hid[:, r, H:2 * H], ACT.Silu).then_inc(silu_done, 1)
                if block_runs(ii, k, RESULT):
                    j = block(ii, k, RESULT)
                    act.wait_ge(yb_done, j + 1)
                    nc.scalar.activation(yw[:, (k - RESULT) % 8, :], y[:, (k - RESULT) % 2, :], ACT.Copy,
                                         scale=weight[:, (k - RESULT) % 8, :]).then_inc(yw_done, 1)

            def lap(ii, count, words=None, ahead=False):
                for k in range(count):
                    block_step(ii, k)

            block_steps(act, lap)

        @program.gpsimd
        def _(pool):
            nc.gpsimd.memset(ident[:], 0.0).then_inc(p_set, 1)
            nc.gpsimd.memset(before[:], 1.0).then_inc(p_set, 1)
            nc.gpsimd.memset(mask_by_b[:], 1.0).then_inc(p_set, 1)
            nc.gpsimd.memset(minus_half[:], -0.5).then_inc(p_set, 1)
            nc.gpsimd.memset(minus_one[:], -1.0).then_inc(p_set, 1)
            nc.gpsimd.memset(eps[:], EPS).then_inc(p_set, 1)
            nc.gpsimd.memset(one[:], 1.0).then_inc(p_set, 1)
            nc.gpsimd.memset(mv[:], 1.0).then_inc(p_set, 1)
            pool.wait_ge(p_set, 8)
            nc.gpsimd.affine_select(out=ident[:], in_=ident[:], compare_op=ALU.not_equal, fill=1.0, base=0,
                                    pattern=[[-1, P]], channel_multiplier=1).then_inc(consts, 1)
            nc.gpsimd.affine_select(out=before[:, 0, :], in_=before[:, 0, :], compare_op=ALU.is_gt, fill=0.0, base=0,
                                    pattern=[[1, P]], channel_multiplier=-1).then_inc(consts, 1)
            nc.gpsimd.affine_select(out=mask_by_b[:], in_=mask_by_b[:], compare_op=ALU.is_ge, fill=0.0, base=0,
                                    pattern=[[-64, 2], [-HD, 8]], channel_multiplier=1).then_inc(p_set, 1)
            pool.wait_ge(p_set, 9)
            nc.gpsimd.affine_select(out=mask_by_b[:], in_=mask_by_b[:], compare_op=ALU.is_ge, fill=0.0, base=HD - 1,
                                    pattern=[[64, 2], [HD, 8]], channel_multiplier=-1).then_inc(p_set, 1)
            nc.gpsimd.iota(iota8[:], [[0, 8], [1, E]], base=0, channel_multiplier=0,
                           allow_small_or_imprecise_dtypes=True).then_inc(p_set, 1)
            nc.gpsimd.iota(home[:], [[2, T], [1, 2]], base=0, channel_multiplier=2 * T,
                           allow_small_or_imprecise_dtypes=True).then_inc(p_set, 1)
            nc.gpsimd.iota(bases[:], [[REGION, E]], base=0, channel_multiplier=0,
                           allow_small_or_imprecise_dtypes=True).then_inc(p_set, 1)
            nc.gpsimd.iota(marks[:], [[P, T]], base=0, channel_multiplier=0,
                           allow_small_or_imprecise_dtypes=True).then_inc(p_set, 1)
            nc.gpsimd.iota(blk_iota[:], [[1, BLOCKS]], base=0, channel_multiplier=0,
                           allow_small_or_imprecise_dtypes=True).then_inc(p_set, 1)
            nc.gpsimd.memset(k_bd[:], 0.0).then_inc(p_set, 1)
            pool.wait_ge(setup_done, 1)

            def scatter(ii, k):
                due = counted(pool, rounds(ii, k, SCATTER, 4) + 1)
                r = (k - SCATTER) % 8
                pool.wait_ge(place_i_s, due)
                pool.wait_ge(home_s, due)
                pool.wait_ge(w1_s, due)
                for slot in range(2):
                    nc.gpsimd.indirect_dma_start(
                        out=rows_dram, out_offset=bass.IndirectOffsetOnAxis(ap=place_i[:, r, slot:slot + 1], axis=0),
                        in_=routed[:, r, slot, :], in_offset=None).then_inc(scat[r], 16)

            def norms(ii, k):
                s = LAP * ii + k
                r = k % 4
                if runs(ii, k, NORM1):
                    pool.wait_ge(agg1, s + 2)
                    if runs(ii, k, 3):
                        pool.wait_ge(xn_ready, s - 2)
                    nc.gpsimd.tensor_tensor(neg_mean[:, r:r + 1], mv[:, r, 0, 0:1], minus_one[:, 0:1],
                                            ALU.mult).then_inc(neg_done, 1)
                if runs(ii, k, WO):
                    pool.wait_ge(agg2, tile(ii, k, WO) + 1)
                    if runs(ii, k, WO + 4):
                        pool.wait_ge(xn2_ready, tile(ii, k, WO) - 3)
                nc.gpsimd.tensor_tensor(var_eps[:, r, :], mv[:, r, :, 1], eps[:], ALU.add).then_inc(eps_done, 1)
                pool.wait_ge(eps_done, s + 2)
                nc.gpsimd.tensor_tensor(rstd[:, r, :], var_eps[:, r, :], minus_half[:], ALU.pow).then_inc(rstd_done, 1)
                if runs(ii, k, NORM1):
                    pool.wait_ge(neg_done, s + 2)
                    pool.wait_ge(rstd_done, s + 2)
                    nc.gpsimd.tensor_tensor(shift1[:, r:r + 1], neg_mean[:, r:r + 1], rstd[:, r, 0:1],
                                            ALU.mult).then_inc(shift_done, 1)

            def step(ii, k):
                if k % 2 and runs(ii, k, 3):
                    n = LAP // 2 * ii + (k - 3) // 2
                    pool.wait_ge(rope_added, n + 1)
                    if runs(ii, k, 5):
                        pool.wait_ge(k_bd_ready, 2 * n)
                    nc.gpsimd.tensor_tensor(k_rot, rope_sum[:], kb_tab[:], ALU.add).then_inc(k_rot_ready, 1)
                if k % 2 == 0 and runs(ii, k, 4):
                    n = LAP // 2 * ii + (k - 4) // 2
                    pool.wait_ge(rope_muld, 2 * n + 2)
                    if runs(ii, k, 6):
                        pool.wait_ge(q_bd_ready, 2 * n)
                    nc.gpsimd.tensor_tensor(q_part[:], rope_mul[:, 0], qb_tab[:], ALU.add).then_inc(q_part_ready, 1)
                if runs(ii, k, SCATTER):
                    scatter(ii, k)
                if groups(ii, k, PLACE):
                    g = rounds(ii, k, PLACE, 4)
                    q = (k - PLACE) % 8
                    pool.wait_ge(odds_s, g + 1)
                    nc.gpsimd.tensor_tensor(odds1[:], odds[:], one[:], ALU.add).then_inc(odds1_s, 1)
                    pool.wait_ge(odds1_s, g + 1)
                    nc.gpsimd.tensor_tensor(share[:], odds1[:], minus_one[:], ALU.pow).then_inc(share_s, 1)
                    pool.wait_ge(share_s, g + 1)
                    nc.gpsimd.tensor_tensor(routed[:, q:q + 4, 0, D], share[:], tgate[:, 1:2].to_broadcast([P, 4]),
                                            ALU.mult).then_inc(w0_s, 1)
                    pool.wait_ge(w0_s, g + 1)
                    nc.gpsimd.tensor_tensor(routed[:, q:q + 4, 1, D], routed[:, q:q + 4, 0, D], odds[:],
                                            ALU.mult).then_inc(w1_s, 1)
                if runs(ii, k, 2):
                    t = tile(ii, k, 2)
                    pool.wait_ge(xn_ready, t + 1)
                    nc.gpsimd.tensor_tensor(x[:, t, :], x[:, t, :], bo_wide, ALU.add).then_inc(xb_ready, 1)
                if runs(ii, k, NORM1) or runs(ii, k, WO):
                    norms(ii, k)

            steps(pool, step)

            def block_step(ii, k):
                if block_runs(ii, k, RESULT):
                    j = block(ii, k, RESULT)
                    r = (k - RESULT) % 8
                    due = counted(pool, j + 1)
                    pool.wait_ge(yw_done, due)
                    pool.wait_ge(home_done, due)
                    nc.gpsimd.indirect_dma_start(
                        out=result_dram, out_offset=bass.IndirectOffsetOnAxis(ap=home_i[:, r, :], axis=0),
                        in_=yw[:, r, :], in_offset=None, bounds_check=2 * TOKENS - 1,
                        oob_is_err=False).then_inc(y_out[r], 16)

            def lap(ii, count, words=None, ahead=False):
                for k in range(count):
                    block_step(ii, k)

            block_steps(pool, lap)

            def finish(lap, k):
                c = 4 * lap + k
                pool.wait_ge(both, c + 1)
                nc.gpsimd.tensor_tensor(x[:, bass.ds(CH * c, CH), :], x[:, bass.ds(CH * c, CH), :],
                                        res[:, k, :, 0], ALU.add).then_inc(fin_done, 1)

            with pool.Fori(0, CHUNKS // 4) as lap:
                for k in range(4):
                    finish(lap, k)

        @program.vector
        def _(dve):
            nc.vector.memset(q_bd[:], 0.0).then_inc(d_set, 1)
            nc.vector.memset(v_bd[:], 0.0).then_inc(d_set, 1)
            nc.vector.memset(turn_ps, 0.0).then_inc(d_set, 1)
            nc.vector.memset(pad_rows[:], 0.0).then_inc(d_set, 1)
            nc.vector.memset(lap_experts_i[:], 0).then_inc(d_set, 1)
            for i in range(8):
                nc.vector.memset(place_value[:, i:i + 1], float(E ** i)).then_inc(lst, 1)
            nc.vector.memset(bv_wide[:], 1.0).then_inc(d_set, 1)
            dve.wait_ge(d_set, 6)
            nc.vector.memset(v_bd[0:64, :, :, :, HD:HD + 1], 1.0).then_inc(d_set, 1)
            nc.vector.memset(v_bd[64:128, :, :, :, 2 * HD + 1:2 * HD + 2], 1.0).then_inc(d_set, 1)
            nc.vector.memset(pad_rows[:, D + 1:D + 2], float(NOWHERE)).then_inc(d_set, 1)
            dve.wait_ge(w_in, 16 * W_LOADS)
            nc.vector.tensor_scalar(bv_wide[:], bv_wide[:], bv_col, None, ALU.mult).then_inc(setup, 1)
            dve.wait_ge(tanh_done, 1)
            nc.vector.tensor_scalar(wo_gated[:], wo, tgate[:, 0:1], None, ALU.mult).then_inc(d_set, 1)
            dve.wait_ge(bias_ps_done, 1)
            nc.vector.tensor_tensor(bo_wide, wo_ps, bo_wide, ALU.add).then_inc(d_set, 1)
            dve.wait_ge(d_set, 11)
            nc.vector.tensor_scalar(bo_wide, bo_wide, tgate[:, 0:1], None, ALU.mult).then_inc(d_set, 1)
            done = 12
            for col, tab in ((qb_col, qb_tab), (kb_col, kb_tab)):
                for u in range(2):
                    nc.vector.tensor_scalar(bt_tmp[:, u, :], turn_tab[:, 0, :], col[:, 0, u:u + 1],
                                            None, ALU.mult).then_inc(d_set, 1)
                    nc.vector.tensor_scalar(tab[:, u, 0, :], turn_tab[:, 1, :], col[:, 1, u:u + 1],
                                            None, ALU.mult).then_inc(d_set, 1)
                done += 4
                dve.wait_ge(d_set, done)
                nc.vector.tensor_tensor(tab[:, :, 1, :], tab[:, :, 0, :], bt_tmp[:], ALU.add).then_inc(d_set, 1)
                dve.wait_ge(d_set, done + 1)
                nc.vector.tensor_copy(tab[:, :, 0, :], tab[:, :, 1, :]).then_inc(d_set, 1)
                done += 2
                dve.wait_ge(d_set, done)
            dve.wait_ge(p_set, 16)
            nc.vector.tensor_tensor(head_mask[:], mask_by_b[:, 0], mask_by_b[:, 1], ALU.add).then_inc(d_set, 1)
            dve.wait_ge(d_set, done + 1)
            nc.vector.tensor_copy(base[:], bases[:]).then_inc(setup_done, 1)
            dve.wait_ge(setup_done, 1)

            def step(ii, k):
                s = LAP * ii + k
                lag = 3 if k % 2 else 4
                if runs(ii, k, lag):
                    n = LAP // 2 * ii + (k - lag) // 2
                    dve.wait_ge(proj_done, s - 2)
                    if k % 2 == 0:
                        dve.wait_ge(rope_added, n + 1)
                    elif runs(ii, k, lag + 2):
                        dve.wait_ge(q_bd_ready, 2 * n)
                    nc.vector.tensor_tensor(
                        rope_mul[:].rearrange("p w u t k -> p w (u t) k"),
                        proj_ps.rearrange("p (w c k) -> p w c k", w=2, k=S),
                        turn_tab.unsqueeze(2).to_broadcast([P, 2, 4, S]), ALU.mult).then_inc(rope_muld, 1)
                if runs(ii, k, NORM1):
                    t = tile(ii, k, NORM1)
                    due = counted(dve, 16 * (rounds(ii, k, NORM1, 4) + 1))
                    dve.wait_ge(x_in[(k - NORM1) % 4], due)
                    nc.vector.bn_stats(stats[:, k % 4, 0, :], x[:, t, :]).then_inc(bn1, 1)
                if k % 2 and runs(ii, k, lag):
                    dve.wait_ge(rope_muld, s - 2)
                    if runs(ii, k, lag + 2):
                        dve.wait_ge(k_rot_ready, n)
                    nc.vector.tensor_tensor(rope_sum[:], rope_mul[:, 0], rope_mul[:, 1], ALU.add).then_inc(rope_added, 1)
                if runs(ii, k, SCORE):
                    t = tile(ii, k, SCORE)
                    r = (k - SCORE) % 2
                    v = score_ps.rearrange("p u (h k) -> p u h k", h=8)
                    dve.wait_ge(score_done, 2 * t + 2)
                    nc.vector.tensor_reduce(peak[:, r], v, AX.X, ALU.max).then_inc(peak_done, 1)
                if runs(ii, k, TOP):
                    due = counted(dve, tile(ii, k, TOP) + 1)
                    dve.wait_ge(lg, due)
                    nc.vector.max(top[:, (k - TOP) % 8, :], logits[:, (k - TOP) % 2, :]).then_inc(topd, 1)
                if runs(ii, k, SCORE):
                    dve.wait_ge(peak_done, t + 1)
                    nc.vector.tensor_tensor(probs[:, r], v, peak[:, r].unsqueeze(3).to_broadcast([P, 2, 8, S]),
                                            ALU.subtract).then_inc(shifted, 1)
                if runs(ii, k, TOP):
                    due = counted(dve, tile(ii, k, TOP) + 1)
                    dve.wait_ge(topd, due)
                    nc.vector.max_index(top_at[:, (k - TOP) % 8, :], top[:, (k - TOP) % 8, :],
                                        logits[:, (k - TOP) % 2, :]).then_inc(topi, 1)
                if runs(ii, k, NORM1):
                    due = counted(dve, tile(ii, k, NORM1) + 1)
                    dve.wait_ge(bn1, due)
                    nc.vector.bn_aggr(mv[:, k % 4, 0, :], stats[:, k % 4, 0, :]).then_inc(agg1, 1)
                if runs(ii, k, XN2):
                    t = tile(ii, k, XN2)
                    r = (k - 1) % 4
                    q = (k - XN2) % 8
                    dve.wait_ge(rstd_done, s + 1)
                    if runs(ii, k, XN2 + 8):
                        dve.wait_ge(scat[q], 32 * rounds(ii, k, XN2, 8))
                    nc.vector.tensor_scalar(routed[:, q, :, 0:D], x[:, t, :].unsqueeze(1).to_broadcast([P, 2, D]),
                                            mv[:, r, 1, 0:1], rstd[:, r, 1:2], ALU.subtract, ALU.mult).then_inc(xn2_ready, 1)
                if k % 2 == 0 and runs(ii, k, lag):
                    dve.wait_ge(q_part_ready, n + 1)
                    if runs(ii, k, lag + 4):
                        dve.wait_ge(score_done, 4 * n - 4)
                    for b in range(2):
                        rows_b = slice(64 * b, 64 * b + 64)
                        nc.vector.tensor_tensor(
                            q_bd[rows_b, (k - lag) // 2 % 2, :, :, b, :],
                            q_part[rows_b].rearrange("p u t k -> p t u k"),
                            rope_mul[rows_b, 1].rearrange("p u t k -> p t u k"), ALU.add).then_inc(q_bd_ready, 1)
                if groups(ii, k, ROUTE):
                    g = rounds(ii, k, ROUTE, 4)
                    q = (k - ROUTE) % 8
                    nc.vector.tensor_tensor(gap[:], top[:, q:q + 4, 1], top[:, q:q + 4, 0], ALU.subtract).then_inc(gap_s, 1)
                    dve.wait_ge(topi, 4 * g + 4)
                    nc.vector.tensor_copy(top_f[:], top_at[:, q:q + 4, 0:2]).then_inc(topf, 1)
                    dve.wait_ge(topf, g + 1)
                    nc.vector.tensor_tensor(chosen[:], iota8[:], top_f[:].unsqueeze(3).to_broadcast([P, 4, 2, E]),
                                            ALU.is_equal).then_inc(chose, 1)
                    dve.wait_ge(chose, g + 1)
                    nc.vector.tensor_tensor(chosen_sum[:], chosen[:, :, 0], chosen[:, :, 1], ALU.add).then_inc(chose_b, 1)
                if runs(ii, k, BACK) or runs(ii, k, WO) or runs(ii, k, GATE) or groups(ii, k, PLACE):
                    dve.wait_ge(misc_done, min(s, T + GATE) - BACK + 1 if isinstance(ii, int) else s - BACK + 1)
                if groups(ii, k, PLACE):
                    g = rounds(ii, k, PLACE, 4)
                    q = (k - PLACE) % 8
                    nc.vector.tensor_tensor(place[:], rank_ps.rearrange("p (t e) -> p t e", e=E),
                                            base[:].unsqueeze(1).to_broadcast([P, 4, E]), ALU.add).then_inc(place_s, 1)
                if runs(ii, k, WO):
                    t = tile(ii, k, WO)
                    dve.wait_ge(xb_ready, t + 1)
                    nc.vector.tensor_tensor(x[:, t, :], wo_ps, x[:, t, :], ALU.add).then_inc(x2_done, 1)
                if runs(ii, k, GATE):
                    nc.vector.tensor_tensor(logits[:, (k - GATE) % 2, :], gate_ps, gate_b, ALU.add).then_inc(lg, 1)
                if groups(ii, k, PLACE):
                    dve.wait_ge(place_s, g + 1)
                    nc.vector.tensor_tensor(base[:], total_ps, base[:], ALU.add).then_inc(base_s, 1)
                if runs(ii, k, BACK):
                    r = (k - BACK) % 2
                    v = back_ps.rearrange("p (j c) -> p j c", c=32)[:, :, 0:2 * (HD + 1)].rearrange(
                        "p j (h c) -> p j h c", c=HD + 1)
                    m = inv[:, r, :].rearrange("p (j h) -> p j h", h=2)
                    nc.vector.reciprocal(m, v[:, :, :, HD]).then_inc(inv_done, 1)
                if runs(ii, k, WO):
                    t = tile(ii, k, WO)
                    due = counted(dve, t + 1)
                    dve.wait_ge(x2_done, due)
                    nc.vector.bn_stats(stats[:, k % 4, 1, :], x[:, t, :]).then_inc(bn2, 1)
                if runs(ii, k, BACK):
                    dve.wait_ge(inv_done, tile(ii, k, BACK) + 1)
                    nc.vector.tensor_tensor(o[:, r, :].rearrange("p (j h c) -> p j h c", h=2, c=HD), v[:, :, :, 0:HD],
                                            m.unsqueeze(3).to_broadcast([P, 8, 2, HD]), ALU.mult).then_inc(o_ready, 1)
                if runs(ii, k, WO):
                    due = counted(dve, tile(ii, k, WO) + 1)
                    dve.wait_ge(bn2, due)
                    nc.vector.bn_aggr(mv[:, k % 4, 1, :], stats[:, k % 4, 1, :]).then_inc(agg2, 1)
                if groups(ii, k, PLACE):
                    tiles = slice(q, q + 4)
                    nc.vector.tensor_tensor(place2[:], chosen[:], place[:].unsqueeze(2).to_broadcast([P, 4, 2, E]),
                                            ALU.mult).then_inc(place2_s, 1)
                    nc.vector.tensor_copy(routed[:, tiles, :, D + 1],
                                          home[:, bass.ds(4 * g, 4), :]).then_inc(home_s, 1)
                    dve.wait_ge(place2_s, g + 1)
                    nc.vector.tensor_reduce(place_f[:], place2[:], AX.X, ALU.add).then_inc(place_f_s, 1)
                    dve.wait_ge(place_f_s, g + 1)
                    nc.vector.tensor_copy(place_i[:, tiles, :], place_f[:]).then_inc(place_i_s, 1)

            steps(dve, step)

            dve.wait_ge(base_s, T // 4)
            nc.vector.tensor_copy(pad_i[:], base[:]).then_inc(pad_ready, 1)
            nc.vector.tensor_tensor(fill[:], base[:], bases[:], ALU.subtract).then_inc(lst, 1)
            dve.wait_ge(lst, 9)
            nc.vector.tensor_tensor(over[:], fill[:].unsqueeze(2).to_broadcast([P, E, T]),
                                    marks[:].unsqueeze(1).to_broadcast([P, E, T]), ALU.is_gt).then_inc(lst, 1)
            dve.wait_ge(lst, 10)
            nc.vector.tensor_reduce(blocks_of[:], over[:], AX.X, ALU.add).then_inc(lst, 1)
            dve.wait_ge(lst, 11)
            nc.vector.tensor_copy(ends[:], blocks_of[:]).then_inc(lst, 1)
            dve.wait_ge(lst, 12)
            n = 12
            src, dst = ends, ends_b
            for hop in (1, 2, 4):
                nc.vector.tensor_copy(dst[:, 0:hop], src[:, 0:hop]).then_inc(lst, 1)
                nc.vector.tensor_tensor(dst[:, hop:E], src[:, hop:E], src[:, 0:E - hop], ALU.add).then_inc(lst, 1)
                n += 2
                dve.wait_ge(lst, n)
                src, dst = dst, src
            nc.vector.tensor_tensor(passed[:], blk_iota[:].unsqueeze(2).to_broadcast([P, BLOCKS, E]),
                                    src[:].unsqueeze(1).to_broadcast([P, BLOCKS, E]), ALU.is_ge).then_inc(lst, 1)
            dve.wait_ge(lst, n + 1)
            nc.vector.tensor_reduce(blk_e[:], passed[:], AX.X, ALU.add).then_inc(lst, 1)
            nc.vector.tensor_tensor(passed_n[:], passed[:], blocks_of[:].unsqueeze(1).to_broadcast([P, BLOCKS, E]),
                                    ALU.mult).then_inc(lst, 1)
            dve.wait_ge(lst, n + 3)
            nc.vector.tensor_reduce(blk_first[:], passed_n[:], AX.X, ALU.add).then_inc(lst, 1)
            nc.vector.tensor_scalar(blk_live[:], blk_e[:], float(E), float(P), ALU.is_lt, ALU.mult).then_inc(lst, 1)
            nc.vector.tensor_scalar(blk_em[:], blk_e[:], float(E - 1), None, ALU.min).then_inc(lst, 1)
            dve.wait_ge(lst, n + 6)
            nc.vector.tensor_tensor(digits[:].rearrange("p (l i) -> p l i", i=8), blk_em[:].rearrange("p (l i) -> p l i", i=8),
                                    place_value[:].unsqueeze(1).to_broadcast([P, BLOCKS // 8, 8]), ALU.mult).then_inc(lst, 1)
            nc.vector.tensor_tensor(blk_rel[:], blk_iota[:], blk_first[:], ALU.subtract).then_inc(lst, 1)
            dve.wait_ge(lst, n + 8)
            nc.vector.tensor_tensor(blk_row[:], blk_rel[:], blk_live[:], ALU.mult).then_inc(lst, 1)
            nc.vector.tensor_reduce(lap_experts[:], digits[:].rearrange("p (l i) -> p l i", i=8), AX.X, ALU.add).then_inc(lst, 1)
            dve.wait_ge(lst, n + 10)
            nc.vector.tensor_copy(lap_experts_i[:, 1:], lap_experts[:]).then_inc(list_ready, 1)
            nc.vector.scalar_tensor_tensor(blk_row_i[:], blk_e[:], float(REGION), blk_row[:],
                                           ALU.mult, ALU.add).then_inc(list_ready, 1)
            dve.wait_ge(list_ready, 2)
            dve.wait_ge(w_in2, 64 * E)

            def block_step(ii, k, expert, hidden_at):
                if block_runs(ii, k, META):
                    j = block(ii, k, META)
                    q = (k - META) % 8
                    dve.wait_ge(rt_done, j + 1)
                    if block_runs(ii, k, META + 8):
                        dve.wait_ge(y_out[q], 16 * (ii + (k - META) // 8))
                    nc.vector.tensor_copy(home_i[:, q, :], rows[:, q, D + 1:D + 2]).then_inc(home_done, 1)
                    nc.vector.tensor_copy(weight[:, q, :], rows[:, q, D:D + 1]).then_inc(weight_done, 1)
                if block_runs(ii, k, GLU):
                    j = block(ii, k, GLU)
                    r = (k - GLU) % 2
                    dve.wait_ge(silu_done, j + 1)
                    if block_runs(ii, k, GLU + 2):
                        dve.wait_ge(at_done, j - 1)
                    nc.vector.tensor_tensor(act_sb[:, r, :], hid[:, r, 0:H], silu[:, r, :], ALU.mult).then_inc(act_done, 1)
                if block_runs(ii, k, HIDDEN):
                    j = block(ii, k, HIDDEN)
                    r = (k - HIDDEN) % 2
                    dve.wait_ge(h_done, j + 1)
                    nc.vector.tensor_tensor(hid[:, r, :], ps[:, r, :], b01[:, bass.ds(hidden_at, 2 * H)],
                                            ALU.add).then_inc(hb_done, 1)
                result_at = next_at = None
                if block_runs(ii, k, RESULT):
                    result_at = nc.snap(expert(k - RESULT) * (D), engines=[mybir.EngineType.DVE])
                if k < 7 and block_runs(ii, k + 1, HIDDEN):
                    next_at = nc.snap(expert(k + 1 - HIDDEN) * (2 * H), engines=[mybir.EngineType.DVE])
                if block_runs(ii, k, RESULT):
                    j = block(ii, k, RESULT)
                    dve.wait_ge(y_done, j + 1)
                    if block_runs(ii, k, RESULT + 2):
                        dve.wait_ge(yw_done, j - 1)
                    nc.vector.tensor_tensor(y[:, (k - RESULT) % 2, :], ps[:, 6 + (k - RESULT) % 2, 0:D], b2[:, bass.ds(result_at, D)],
                                            ALU.add).then_inc(yb_done, 1)

                return next_at

            def lap(ii, count, words=None, ahead=False):
                words = words or last_and_this_lap(mybir.EngineType.DVE, ii)
                expert, next_words = experts_near(words), (words[1], None)
                hidden_at = expert(-HIDDEN) * (2 * H) if block_runs(ii, 0, HIDDEN) else None
                for k in range(count):
                    hidden_at = block_step(ii, k, expert, hidden_at)
                    if ahead and k == 4 and block_runs(ii, 8, ROWS_T):
                        next_words = (words[1], lap_word(mybir.EngineType.DVE, ii + 1))
                return next_words

            block_steps(dve, lap)

            def add_both(lap, k):
                dve.wait_ge(res_in[k], 16 * lap + 16)
                nc.vector.tensor_tensor(res[:, k, :, 0], res[:, k, :, 0], res[:, k, :, 1], ALU.add).then_inc(both, 1)

            with dve.Fori(0, CHUNKS // 4) as lap:
                for k in range(4):
                    add_both(lap, k)


def kernel(**inputs):
    import numpy as _np
    import concourse.bacc as _bacc
    from concourse.bass_utils import run_bass_kernel_spmd as _run

    g = {n: _np.asarray(v) for n, v in inputs.items()}
    half_swap = (_np.arange(D) // HD) * HD + (_np.arange(D) % HD + HD // 2) % HD
    spread = _np.arange(D).reshape(NH // 2, 2, HD).transpose(1, 0, 2).ravel()

    def plain_and_swapped(w):
        return _np.stack([w.T, w[half_swap].T], axis=1)

    def bias_columns(b):
        return _np.stack([b, b[half_swap]]).reshape(2, 2, 64).transpose(2, 0, 1)

    inv_freq = (1.0 / _np.float32(10000.0) ** (_np.arange(0, HD, 2, dtype=_np.float32) / _np.float32(HD))).astype(_np.float32)
    angle = _np.arange(S, dtype=_np.float32)[None, :] * inv_freq[_np.arange(P) % (HD // 2)][:, None]
    sign = _np.where(_np.arange(P) % HD < HD // 2, -1.0, 1.0).astype(_np.float32)[:, None]
    turn = _np.stack([_np.cos(angle), _np.sin(angle) * sign], axis=1).astype(_np.float32)

    w0, w1, w2 = g["L0_ffn_w0"], g["L0_ffn_w1"], g["L0_ffn_w2"]
    qb, kb = bias_columns(g["L0_xattn_bq"]), bias_columns(g["L0_xattn_bk"])
    by_row = [plain_and_swapped(g["L0_xattn_Wk"]), plain_and_swapped(g["L0_xattn_Wq"]), g["L0_xattn_Wv"].T[:, spread],
              g["L0_xattn_Wo"].T, turn, g["L0_ffn_gate_w"].T, _np.tile(kb, (2, 1, 1)), _np.tile(qb, (2, 1, 1)),
              g["L0_xattn_bv"][:, None]]
    arrays = {
        "x": g["x"], "ctx_1024": g["ctx_1024"],
        "by_row": _np.concatenate([v.reshape(D, -1) for v in by_row], axis=1),
        "alike": _np.concatenate([g["L0_xattn_bo"], g["L0_ffn_gate_b"], g["g_xattn"], g["g_ffn"]]),
        "w01": _np.stack([w0, w1]).transpose(3, 1, 0, 2).reshape(D, -1),
        "b01": _np.stack([g["L0_ffn_b0"], g["L0_ffn_b1"]], axis=1).reshape(-1),
        "w2": w2.reshape(E, D, 2, H // 2).transpose(3, 0, 2, 1).reshape(H // 2, -1),
        "b2": g["L0_ffn_b2"].reshape(-1),
    }
    nc = _bacc.Bacc("TRN2", target_bir_lowering=False, num_devices=1)
    feeds, handles = {}, {}
    for name, v in arrays.items():
        v = _np.ascontiguousarray(v)
        feeds[f"in_{name}"] = v
        handles[name] = nc.dram_tensor(f"in_{name}", v.shape, mybir.dt.from_np(v.dtype), kind="ExternalInput").ap()
    out = nc.dram_tensor("out_0", (B, S, D), F32, kind="ExternalOutput").ap()
    flamingo_block(nc, handles, out)
    return _run(nc, [feeds], core_ids=[0]).results[0]["out_0"]
```
